# Optimizing a Trainium2 kernel written in Bass

```python
import numpy as np
import jax
import jax.numpy as jnp

def _softmax(x, axis=-1):
    return jax.nn.softmax(x, axis=axis)

def _gelu(x):
    return jax.nn.gelu(x, approximate=True)

def _silu(x):
    return jax.nn.silu(x)

def _sigmoid(x):
    return jax.nn.sigmoid(x)

def _layernorm(x, axis=-1, eps=1e-05):
    m = jnp.mean(x, axis=axis, keepdims=True)
    v = jnp.var(x, axis=axis, keepdims=True)
    return (x - m) / jnp.sqrt(v + eps)

def _scatter_add(tgt, idx, src, axis=0):
    return tgt.at[idx].add(src)

def _segment_sum(src, seg, n):
    return jax.ops.segment_sum(src, seg, n)
kernel_name = 'mk_flamingo_gated_d2_seqx_r4_d65cb6'

def setup_inputs(seed: int=0):
    np.random.seed(seed)
    _w = jnp.asarray

    def _rec_inputs():
        import jax
        import jax.numpy as jnp
        _rk = jax.random.key(seed)
        x = -0.0002928 + 1 * jax.random.normal(jax.random.fold_in(_rk, 1), (64, 128, 256), jnp.float32)
        _lenS = 128 - jax.random.randint(jax.random.fold_in(_rk, 7), (64,), 0, max(1, 128 // 4) + 1, jnp.int32)
        _lenS2 = 128 - jax.random.randint(jax.random.fold_in(_rk, 8), (64,), 0, max(1, 128 // 4) + 1, jnp.int32)
        _ctx_1024P = jax.random.normal(jax.random.fold_in(_rk, 11), (64, 16, 256), jnp.float32)
        _ctx_1024c = jax.random.dirichlet(jax.random.fold_in(_rk, 511), 0.3 * jnp.ones((16,), jnp.float32), (64, 128))
        _ctx_1024t = jnp.einsum('bsk,bkd->bsd', _ctx_1024c, _ctx_1024P)
        _ctx_1024t = _ctx_1024t * jax.lax.rsqrt(jnp.mean(jnp.square(_ctx_1024t)) + 1e-12) * 0.953939
        ctx_1024 = -1.39393e-06 + 0.999914 * (_ctx_1024t + 0.3 * jax.random.normal(jax.random.fold_in(_rk, 611), (64, 128, 256), jnp.float32))
        _validS = jnp.arange(128)[None, :] < _lenS[:, None]
        _validS2 = jnp.arange(128)[None, :] < _lenS2[:, None]
        _causal = jnp.tril(jnp.ones((128, 128), dtype=bool))
        mask_1x1xSxS2_ik0 = jnp.where(jnp.broadcast_to(_validS2[0:1, None, None, :], (1, 1, 128, 128)), 0, 1).astype(jnp.int32)
        _g = jax.random.normal(jax.random.fold_in(_rk, 9001), (2, 2), jnp.float32)
        _g = jnp.sign(_g) * jnp.maximum(jnp.abs(_g), 1.0) + (_g == 0) * 1.0
        g_xattn = _g[0]
        g_ffn = _g[1]
        return (x, ctx_1024, mask_1x1xSxS2_ik0, g_xattn, g_ffn)
    x, ctx_1024, mask_1x1xSxS2_ik0, g_xattn, g_ffn = _rec_inputs()

    def _L0_xattn_setup():
        import jax, jax.numpy as jnp
        import numpy as np
        B, T, D, H = (2, 512, 256, 16)
        DH = D // H
        key = jax.random.key(seed)
        ks = jax.random.split(key, 11)
        s = 1.0 / np.sqrt(D)
        return {'q': jax.random.normal(ks[0], (B, T, D), jnp.float32), 'k': jax.random.normal(ks[1], (B, T, D), jnp.float32), 'v': jax.random.normal(ks[2], (B, T, D), jnp.float32), 'wq_w': jax.random.normal(ks[3], (D, D), jnp.float32) * s, 'wq_b': jnp.zeros((D,), jnp.float32), 'wk_w': jax.random.normal(ks[4], (D, D), jnp.float32) * s, 'wk_b': jnp.zeros((D,), jnp.float32), 'wv_w': jax.random.normal(ks[5], (D, D), jnp.float32) * s, 'wv_b': jnp.zeros((D,), jnp.float32), 'wo_w': jax.random.normal(ks[6], (D, D), jnp.float32) * s, 'wo_b': jnp.zeros((D,), jnp.float32)}
    _L0_xattn_all = _L0_xattn_setup()
    _L0_xattn_in = {k: v for k, v in _L0_xattn_all.items() if k in ('wq_w', 'wq_b', 'wk_w', 'wk_b', 'wv_w', 'wv_b', 'wo_w', 'wo_b')}
    del _L0_xattn_all

    def _L0_ffn_setup():
        import jax, jax.numpy as jnp
        import numpy as np
        E, K, NG, TG = (64, 8, 8, 4)
        CAP = 256
        SCALE = 2.5

        def _route(x_flat, gate_weight, e_bias):
            T = x_flat.shape[0]
            logits = x_flat.astype(jnp.float32) @ gate_weight.astype(jnp.float32).T
            scores = jax.nn.sigmoid(logits)
            sfc = scores + e_bias[None, :]
            group_scores = jax.lax.top_k(sfc.reshape(T, NG, E // NG), 2)[0].sum(-1)
            _, gidx = jax.lax.top_k(group_scores, TG)
            gmask = jnp.zeros((T, NG), jnp.float32).at[jnp.arange(T)[:, None], gidx].set(1.0)
            smask = jnp.repeat(gmask, E // NG, axis=1)
            tmp = jnp.where(smask > 0, sfc, 0.0)
            _, topk_idx = jax.lax.top_k(tmp, K)
            topk_w = jnp.take_along_axis(scores, topk_idx, axis=1)
            topk_w = topk_w / (topk_w.sum(-1, keepdims=True) + 1e-20)
            return (topk_idx, topk_w * SCALE)

        def _moe_forward(hidden_states, gate_weight, e_bias, w1, w2, w3, shared_gate, shared_up, shared_down):
            B, S, H = hidden_states.shape
            T = B * S
            x = hidden_states.reshape(T, H)
            topk_idx, topk_w = _route(x, gate_weight, e_bias)
            Sk = T * K
            flat_e = topk_idx.reshape(-1)
            order = jnp.argsort(flat_e)
            sorted_e = flat_e[order]
            counts = jax.ops.segment_sum(jnp.ones((Sk,), jnp.int32), flat_e, num_segments=E)
            offsets = jnp.cumsum(counts) - counts
            pos = jnp.arange(Sk) - offsets[sorted_e]
            tok_sorted = x[order // K]
            xe = jnp.zeros((E, CAP, H), x.dtype).at[sorted_e, pos].set(tok_sorted, mode='drop')
            h = jax.nn.silu(jnp.einsum('ech,efh->ecf', xe, w1)) * jnp.einsum('ech,efh->ecf', xe, w3)
            ye = jnp.einsum('ecf,ehf->ech', h, w2)
            pos_c = jnp.minimum(pos, CAP - 1)
            vals = ye[sorted_e, pos_c]
            vals = jnp.where((pos < CAP)[:, None], vals, 0.0)
            flat_w = topk_w.reshape(-1)[order].astype(vals.dtype)
            flat_t = (jnp.arange(Sk) // K)[order]
            out = jax.ops.segment_sum(vals * flat_w[:, None], flat_t, num_segments=T)
            shared = jax.nn.silu(x @ shared_gate.T) * (x @ shared_up.T) @ shared_down.T
            return (out + shared).reshape(B, S, H)
        key = jax.random.key(seed)
        ks = jax.random.split(key, 9)
        B, S, H, F = (1, 512, 256, 128)
        bound = 1.0 / 32.0
        return {'hidden_states': jax.random.normal(ks[0], (B, S, H), jnp.float32), 'gate_weight': jax.random.uniform(ks[1], (E, H), jnp.float32, -bound, bound), 'e_bias': jnp.zeros((E,), jnp.float32), 'w1': jax.random.normal(ks[2], (E, F, H), jnp.float32) * 0.02, 'w2': jax.random.normal(ks[3], (E, H, F), jnp.float32) * 0.02, 'w3': jax.random.normal(ks[4], (E, F, H), jnp.float32) * 0.02, 'shared_gate': jax.random.normal(ks[5], (2 * F, H), jnp.float32) * 0.02, 'shared_up': jax.random.normal(ks[6], (2 * F, H), jnp.float32) * 0.02, 'shared_down': jax.random.normal(ks[7], (H, 2 * F), jnp.float32) * 0.02}
    _L0_ffn_all = _L0_ffn_setup()
    _L0_ffn_in = {k: v for k, v in _L0_ffn_all.items() if k in ('gate_weight', 'e_bias', 'w1', 'w2', 'w3', 'shared_gate', 'shared_up', 'shared_down')}
    del _L0_ffn_all

    def _L1_xattn_setup():
        import jax, jax.numpy as jnp
        import numpy as np
        import math
        B, S, D, H = (2, 512, 256, 16)
        DK = D // H

        def _split_heads(x):
            b, s, _ = x.shape
            return x.reshape(b, s, H, DK).transpose(0, 2, 1, 3)
        key = jax.random.key(seed)
        ks = jax.random.split(key, 12)
        std = 1.0 / math.sqrt(D)
        inp = {'q': jax.random.normal(ks[0], (B, S, D), jnp.float32), 'k': jax.random.normal(ks[1], (B, S, D), jnp.float32), 'v': jax.random.normal(ks[2], (B, S, D), jnp.float32), 'mask': jnp.tril(jnp.ones((S, S), jnp.int32))[None, None, :, :], 'wq': jax.random.normal(ks[3], (D, D), jnp.float32) * std, 'bq': jax.random.normal(ks[4], (D,), jnp.float32) * std, 'wk': jax.random.normal(ks[5], (D, D), jnp.float32) * std, 'bk': jax.random.normal(ks[6], (D,), jnp.float32) * std, 'wv': jax.random.normal(ks[7], (D, D), jnp.float32) * std, 'bv': jax.random.normal(ks[8], (D,), jnp.float32) * std, 'wo': jax.random.normal(ks[9], (D, D), jnp.float32) * std, 'bo': jax.random.normal(ks[10], (D,), jnp.float32) * std}
        return inp
    _L1_xattn_all = _L1_xattn_setup()
    _L1_xattn_in = {k: v for k, v in _L1_xattn_all.items() if k in ('wq', 'bq', 'wk', 'bk', 'wv', 'bv', 'wo', 'bo')}
    del _L1_xattn_all

    def _L1_ffn_setup():
        import jax, jax.numpy as jnp
        import numpy as np
        QMAX = 127.0

        def _ste_round(v):
            return v + jax.lax.stop_gradient(jnp.round(v) - v)

        def _act_fake_quant(x, clip_factor):
            scale = jax.nn.sigmoid(clip_factor) * jnp.max(jnp.abs(x)) / QMAX
            return jnp.clip(_ste_round(x / scale), -QMAX - 1.0, QMAX) * scale

        def _weight_fake_quant(w):
            scale = jnp.max(jnp.abs(w), axis=1, keepdims=True) / QMAX
            return jnp.clip(_ste_round(w / scale), -QMAX - 1.0, QMAX) * scale
        key = jax.random.key(seed)
        k1, k2, k3, k4 = jax.random.split(key, 4)
        B, S, H, I = (8, 2048, 256, 704)
        return {'x': jax.random.normal(k1, (B, S, H), dtype=jnp.float32), 'clip_x': jnp.full((1,), 4.0, dtype=jnp.float32), 'clip_down': jnp.full((1,), 4.0, dtype=jnp.float32), 'w_gate': jax.random.normal(k2, (I, H), dtype=jnp.float32) * 0.02, 'w_up': jax.random.normal(k3, (I, H), dtype=jnp.float32) * 0.02, 'w_down': jax.random.normal(k4, (H, I), dtype=jnp.float32) * 0.02}
    _L1_ffn_all = _L1_ffn_setup()
    _L1_ffn_in = {k: v for k, v in _L1_ffn_all.items() if k in ('clip_x', 'clip_down', 'w_gate', 'w_up', 'w_down')}
    del _L1_ffn_all
    return {'x': x, 'ctx_1024': ctx_1024, 'mask_1x1xSxS2_ik0': mask_1x1xSxS2_ik0, 'g_xattn': g_xattn, 'g_ffn': g_ffn, 'L0_xattn_wq_w': _L0_xattn_in['wq_w'], 'L0_xattn_wq_b': _L0_xattn_in['wq_b'], 'L0_xattn_wk_w': _L0_xattn_in['wk_w'], 'L0_xattn_wk_b': _L0_xattn_in['wk_b'], 'L0_xattn_wv_w': _L0_xattn_in['wv_w'], 'L0_xattn_wv_b': _L0_xattn_in['wv_b'], 'L0_xattn_wo_w': _L0_xattn_in['wo_w'], 'L0_xattn_wo_b': _L0_xattn_in['wo_b'], 'L0_ffn_gate_weight': _L0_ffn_in['gate_weight'], 'L0_ffn_e_bias': _L0_ffn_in['e_bias'], 'L0_ffn_w1': _L0_ffn_in['w1'], 'L0_ffn_w2': _L0_ffn_in['w2'], 'L0_ffn_w3': _L0_ffn_in['w3'], 'L0_ffn_shared_gate': _L0_ffn_in['shared_gate'], 'L0_ffn_shared_up': _L0_ffn_in['shared_up'], 'L0_ffn_shared_down': _L0_ffn_in['shared_down'], 'L1_xattn_wq': _L1_xattn_in['wq'], 'L1_xattn_bq': _L1_xattn_in['bq'], 'L1_xattn_wk': _L1_xattn_in['wk'], 'L1_xattn_bk': _L1_xattn_in['bk'], 'L1_xattn_wv': _L1_xattn_in['wv'], 'L1_xattn_bv': _L1_xattn_in['bv'], 'L1_xattn_wo': _L1_xattn_in['wo'], 'L1_xattn_bo': _L1_xattn_in['bo'], 'L1_ffn_clip_x': _L1_ffn_in['clip_x'], 'L1_ffn_clip_down': _L1_ffn_in['clip_down'], 'L1_ffn_w_gate': _L1_ffn_in['w_gate'], 'L1_ffn_w_up': _L1_ffn_in['w_up'], 'L1_ffn_w_down': _L1_ffn_in['w_down']}

def reference(x, ctx_1024, mask_1x1xSxS2_ik0, g_xattn, g_ffn, L0_xattn_wq_w, L0_xattn_wq_b, L0_xattn_wk_w, L0_xattn_wk_b, L0_xattn_wv_w, L0_xattn_wv_b, L0_xattn_wo_w, L0_xattn_wo_b, L0_ffn_gate_weight, L0_ffn_e_bias, L0_ffn_w1, L0_ffn_w2, L0_ffn_w3, L0_ffn_shared_gate, L0_ffn_shared_up, L0_ffn_shared_down, L1_xattn_wq, L1_xattn_bq, L1_xattn_wk, L1_xattn_bk, L1_xattn_wv, L1_xattn_bv, L1_xattn_wo, L1_xattn_bo, L1_ffn_clip_x, L1_ffn_clip_down, L1_ffn_w_gate, L1_ffn_w_up, L1_ffn_w_down):
    import jax
    import jax.numpy as jnp

    def _L0_xattn_ref(q, k, v, wq_w, wq_b, wk_w, wk_b, wv_w, wv_b, wo_w, wo_b):
        import jax, jax.numpy as jnp
        import numpy as np
        B, T, D, H = (2, 512, 256, 16)
        DH = D // H
        b, t, d = q.shape
        wq = (q @ wq_w.T + wq_b).reshape(b, t, H, DH)
        wk = (k @ wk_w.T + wk_b).reshape(b, t, H, DH)
        wv = (v @ wv_w.T + wv_b).reshape(b, t, H, DH)
        scores = jnp.einsum('bthd,bshd->bhts', wq, wk) / jnp.sqrt(jnp.float32(DH))
        probs = jax.nn.softmax(scores, axis=-1)
        attn = jnp.einsum('bhts,bshd->bthd', probs, wv)
        attn = attn.reshape(b, t, d)
        return attn @ wo_w.T + wo_b

    def _L0_ffn_ref(hidden_states, gate_weight, e_bias, w1, w2, w3, shared_gate, shared_up, shared_down):
        import jax, jax.numpy as jnp
        import numpy as np
        E, K, NG, TG = (64, 8, 8, 4)
        CAP = 256
        SCALE = 2.5

        def _route(x_flat, gate_weight, e_bias):
            T = x_flat.shape[0]
            logits = x_flat.astype(jnp.float32) @ gate_weight.astype(jnp.float32).T
            scores = jax.nn.sigmoid(logits)
            sfc = scores + e_bias[None, :]
            group_scores = jax.lax.top_k(sfc.reshape(T, NG, E // NG), 2)[0].sum(-1)
            _, gidx = jax.lax.top_k(group_scores, TG)
            gmask = jnp.zeros((T, NG), jnp.float32).at[jnp.arange(T)[:, None], gidx].set(1.0)
            smask = jnp.repeat(gmask, E // NG, axis=1)
            tmp = jnp.where(smask > 0, sfc, 0.0)
            _, topk_idx = jax.lax.top_k(tmp, K)
            topk_w = jnp.take_along_axis(scores, topk_idx, axis=1)
            topk_w = topk_w / (topk_w.sum(-1, keepdims=True) + 1e-20)
            return (topk_idx, topk_w * SCALE)

        def _moe_forward(hidden_states, gate_weight, e_bias, w1, w2, w3, shared_gate, shared_up, shared_down):
            B, S, H = hidden_states.shape
            T = B * S
            x = hidden_states.reshape(T, H)
            topk_idx, topk_w = _route(x, gate_weight, e_bias)
            Sk = T * K
            flat_e = topk_idx.reshape(-1)
            order = jnp.argsort(flat_e)
            sorted_e = flat_e[order]
            counts = jax.ops.segment_sum(jnp.ones((Sk,), jnp.int32), flat_e, num_segments=E)
            offsets = jnp.cumsum(counts) - counts
            pos = jnp.arange(Sk) - offsets[sorted_e]
            tok_sorted = x[order // K]
            xe = jnp.zeros((E, CAP, H), x.dtype).at[sorted_e, pos].set(tok_sorted, mode='drop')
            h = jax.nn.silu(jnp.einsum('ech,efh->ecf', xe, w1)) * jnp.einsum('ech,efh->ecf', xe, w3)
            ye = jnp.einsum('ecf,ehf->ech', h, w2)
            pos_c = jnp.minimum(pos, CAP - 1)
            vals = ye[sorted_e, pos_c]
            vals = jnp.where((pos < CAP)[:, None], vals, 0.0)
            flat_w = topk_w.reshape(-1)[order].astype(vals.dtype)
            flat_t = (jnp.arange(Sk) // K)[order]
            out = jax.ops.segment_sum(vals * flat_w[:, None], flat_t, num_segments=T)
            shared = jax.nn.silu(x @ shared_gate.T) * (x @ shared_up.T) @ shared_down.T
            return (out + shared).reshape(B, S, H)
        return _moe_forward(hidden_states, gate_weight, e_bias, w1, w2, w3, shared_gate, shared_up, shared_down)

    def _L1_xattn_ref(q, k, v, mask, wq, bq, wk, bk, wv, bv, wo, bo):
        import jax, jax.numpy as jnp
        import numpy as np
        import math
        B, S, D, H = (2, 512, 256, 16)
        DK = D // H

        def _split_heads(x):
            b, s, _ = x.shape
            return x.reshape(b, s, H, DK).transpose(0, 2, 1, 3)
        query = _split_heads(q @ wq.T + bq)
        key_h = _split_heads(k @ wk.T + bk)
        value = _split_heads(v @ wv.T + bv)
        scale = 1.0 / math.sqrt(DK)
        scores = jnp.einsum('bhqd,bhkd->bhqk', query, key_h) * scale
        scores = jnp.where(mask == 0, jnp.float32(-1000000000.0), scores)
        attn = jax.nn.softmax(scores, axis=-1)
        x = jnp.einsum('bhqk,bhkd->bhqd', attn, value)
        x = x.transpose(0, 2, 1, 3).reshape(q.shape[0], -1, H * DK)
        return x @ wo.T + bo

    def _L1_ffn_ref(x, clip_x, clip_down, w_gate, w_up, w_down):
        import jax, jax.numpy as jnp
        import numpy as np
        QMAX = 127.0

        def _ste_round(v):
            return v + jax.lax.stop_gradient(jnp.round(v) - v)

        def _act_fake_quant(x, clip_factor):
            scale = jax.nn.sigmoid(clip_factor) * jnp.max(jnp.abs(x)) / QMAX
            return jnp.clip(_ste_round(x / scale), -QMAX - 1.0, QMAX) * scale

        def _weight_fake_quant(w):
            scale = jnp.max(jnp.abs(w), axis=1, keepdims=True) / QMAX
            return jnp.clip(_ste_round(w / scale), -QMAX - 1.0, QMAX) * scale
        xq = _act_fake_quant(x, clip_x[0])
        gate = jnp.einsum('bsh,ih->bsi', xq, _weight_fake_quant(w_gate))
        up = jnp.einsum('bsh,ih->bsi', xq, _weight_fake_quant(w_up))
        h = _act_fake_quant(jax.nn.silu(gate) * up, clip_down[0])
        return jnp.einsum('bsi,hi->bsh', h, _weight_fake_quant(w_down))
    x = x + jnp.tanh(g_xattn[0]) * _L0_xattn_ref(_layernorm(x, axis=-1), ctx_1024, ctx_1024, L0_xattn_wq_w, L0_xattn_wq_b, L0_xattn_wk_w, L0_xattn_wk_b, L0_xattn_wv_w, L0_xattn_wv_b, L0_xattn_wo_w, L0_xattn_wo_b)
    x = x + jnp.tanh(g_ffn[0]) * _L0_ffn_ref(_layernorm(x, axis=-1), L0_ffn_gate_weight, L0_ffn_e_bias, L0_ffn_w1, L0_ffn_w2, L0_ffn_w3, L0_ffn_shared_gate, L0_ffn_shared_up, L0_ffn_shared_down)
    x = x + jnp.tanh(g_xattn[1]) * _L1_xattn_ref(_layernorm(x, axis=-1), ctx_1024, ctx_1024, mask_1x1xSxS2_ik0, L1_xattn_wq, L1_xattn_bq, L1_xattn_wk, L1_xattn_bk, L1_xattn_wv, L1_xattn_bv, L1_xattn_wo, L1_xattn_bo)
    x = x + jnp.tanh(g_ffn[1]) * _L1_ffn_ref(_layernorm(x, axis=-1), L1_ffn_clip_x, L1_ffn_clip_down, L1_ffn_w_gate, L1_ffn_w_up, L1_ffn_w_down)
    return x

_drawn_inputs = setup_inputs


def setup_inputs(seed=0):
    import zlib

    import numpy as np

    out = dict(_drawn_inputs(seed))
    spreads = {'g_ffn': (-1.0, 0.6),
     'L0_xattn_wq_b': (0.0, 0.559),
     'L0_xattn_wk_b': (0.0, 2.0),
     'L0_xattn_wv_b': (0.0, 0.1),
     'L0_xattn_wo_b': (0.0, 0.1),
     'L0_ffn_e_bias': (0.0, 0.8)}
    factors = {'L0_ffn_gate_weight': 8.0,
     'L0_ffn_w1': 8.0,
     'L0_ffn_w2': 8.0,
     'L0_ffn_w3': 8.0,
     'L0_ffn_shared_gate': 5.249,
     'L0_ffn_shared_up': 5.188,
     'L0_ffn_shared_down': 5.186,
     'L1_ffn_w_gate': 2.878,
     'L1_ffn_w_up': 2.787,
     'L1_ffn_w_down': 2.779,
     'L1_xattn_bv': 2.73}
    for name, (base, spread) in spreads.items():
        noise = np.random.default_rng([zlib.crc32(name.encode()), seed]).standard_normal(out[name].shape)
        drawn = base * np.exp(spread * noise) if base else spread * noise
        out[name] = jnp.asarray(drawn.astype(out[name].dtype))
    for name, factor in factors.items():
        out[name] = (out[name] * factor).astype(out[name].dtype)
    return out
```

```python
import concourse.bass as bass
from concourse import mybir
from contextlib import ExitStack


def flamingo_gated_two_layers(nc: bass.Bass, a, out: bass.AP):
    f32, bf16, i32 = mybir.dt.float32, mybir.dt.bfloat16, mybir.dt.int32
    ALU = mybir.AluOpType
    ACT = mybir.ActivationFunctionType
    AX = mybir.AxisListType.X

    NB, S, D = a["x"].shape
    P = 128
    H = 16
    DH = D // H
    KC = D // P
    HB = P // DH
    GH = 4
    NG = H // GH
    SM_SCALE = float(DH) ** -0.5
    EPS = 1e-5
    T = NB * S
    E, F = a["L0_ffn_w1"].shape[0], a["L0_ffn_w1"].shape[2]
    CAP, TOPK, EG, GSEL, ROUTE_SCALE = 256, 8, 8, 4, 2.5
    EPG = E // EG
    HALVES = CAP // P
    FS = a["L0_ffn_shared_gate"].shape[1]
    ROW = D + E + 4
    TOKC = D + E
    DUMP = T
    I = a["L1_ffn_w_gate"].shape[0]
    IC = (I + P - 1) // P
    IFULL, IREST = I // P, I % P
    CT = 512
    NC_ = T // CT
    TPC = CT // P
    QMAX = 127.0
    RND = 12582912.0
    NEG = -(2.0 ** 60)
    LOW = -1.0e30

    SLOT0, LAGS, UNROLL = 8, 5, 4
    LOOP_END = SLOT0 + max(0, (NB - 2 - SLOT0) // UNROLL * UNROLL)

    xe = nc.dram_tensor("expert_rows", [E * CAP, ROW], f32).ap()
    acc = [nc.dram_tensor(f"accumulator_{n}", [T + HALVES * P, D], f32).ap() for n in range(2)]

    ctx = ExitStack()
    with ctx:
        region = [ctx]

        def sb(name, shape, dt=f32):
            return region[0].enter_context(nc.sbuf_tensor(name, shape, dt))

        def ring(name, n, shape, dt=f32):
            return [sb(f"{name}{k}", shape, dt) for k in range(n)]

        sems = {}

        def sem(name):
            if name not in sems:
                sems[name] = ctx.enter_context(nc.semaphore(name))
            return sems[name]

        bank = [ctx.enter_context(nc.psum_tensor(f"bank{k}", [P, 512], f32)) for k in range(8)]

        ident = sb("ident", [P, P])
        identb = sb("identb", [P, P], bf16)
        strict_tri = sb("strict_tri", [P, P], bf16)
        onesb = sb("onesb", [P, P], bf16)
        gates = sb("gates", [P, 4])
        tg = sb("tg", [P, 4])
        tg_half = sb("tg_half", [P, 1])
        tg_route = sb("tg_route", [P, 1])
        eps_col = sb("eps_col", [P, 1])
        ebias = sb("ebias", [P, E])
        slot_base = sb("slot_base", [P, E])
        slot_base_i = sb("slot_base_i", [P, E], i32)
        tok_i = sb("tok_i", [P, 2], i32)
        mask_i = sb("mask_i", [P, S], i32)
        mask_bias = sb("mask_bias", [P, S], bf16)

        clips = sb("clips", [P, 2])
        sig = sb("sig", [P, 2])
        amax = sb("amax", [P, 2])
        gmax = sb("gmax", [P, 2])
        scl = sb("scl", [P, 5])
        hmax = sb("hmax", [P, 2, IC])
        res = sb("res", [P, NB, D])

        moe_region = ExitStack()
        region[0] = moe_region
        zt = sb("zt", [P, HALVES, ROW])
        w_gate = sb("w_gate", [P, KC, E])
        w_sg, w_su = sb("w_sg", [P, KC, FS]), sb("w_su", [P, KC, FS])
        w_sd = sb("w_sd", [P, FS // P, D])
        pay = ring("pay", 4, [P, ROW])
        x2t = ring("x2t", 2, [P, KC, P])
        en = ring("en", 2, [P, E])
        th = ring("th", 2, [P, FS])
        hs = sb("hs", [P, FS])
        ht = ring("ht", 2, [P, FS // P, P])
        sfc, score, tmp, rep = (sb(n, [P, E]) for n in ("sfc", "score", "tmp", "rep"))
        sel = ring("sel", 2, [P, E], bf16)
        self_ = sb("self_", [P, E])
        wun = sb("wun", [P, E])
        wsum = sb("wsum", [P, 1])
        m8 = sb("m8", [P, EG, 8])
        gs = sb("gs", [P, EG + 4])
        top = sb("top", [P, 8])
        tog = sb("tog", [P, 8])
        grep = sb("grep", [P, EG + 4])
        gmask = sb("gmask", [P, EG, 1])
        count = sb("count", [P, E])
        pos, key, valid = (sb(n, [P, E]) for n in ("pos", "key", "valid"))
        keys8 = sb("keys8", [P, 8])
        far = sb("far", [P, 8])
        idx = ring("idx", 4, [P, TOPK], i32)
        xa = ring("xa", 2, [P, D])

        wa = ring("wa", 2, [P, KC, F])
        wb = ring("wb", 2, [P, KC, F])
        wc = ring("wc", 2, [P, D])
        xr = ring("xr", 2, [P, HALVES, ROW])
        xrt = ring("xrt", 2, [P, KC, CAP])
        sg = ring("sg", 2, [P, CAP])
        he = ring("he", 2, [P, CAP])
        ye = ring("ye", 2, [P, HALVES, D])
        wcol = ring("wcol", 2, [P, HALVES])
        tid = ring("tid", 2, [P, HALVES], i32)

        moe_region.close()
        region[0] = ctx
        MOE_BYTES = 60 * 1024
        big = sb("big", [P, max(NB * D, MOE_BYTES // 4)])
        xn3 = big[:, 0:NB * D].rearrange("p (b d) -> p b d", b=NB)
        attention_region = ExitStack()
        region[0] = attention_region
        w_q, w_k, w_v, w_o = (sb(f"w_{n}", [P, KC, D]) for n in "qkvo")
        qk_bias = sb("qk_bias", [P, 2 * KC])
        v_bias = sb("v_bias", [P, D])
        o_bias = sb("o_bias", [P, D])

        cx = ring("cx", 2, [P, D])
        ax = ring("ax", 2, [P, 2, D])
        xn = ring("xn", 2, [P, D])
        xt = ring("xt", 2, [P, 2 * KC, P])
        qk = ring("qk", 2, [P, 2 * KC, P])
        kbd = ring("kbd", 2, [P, KC, HB * P])
        vx = ring("vx", 2, [P, H, 32])
        sc = ring("sc", 4, [P, GH, P])
        pt = ring("pt", 2, [P, GH, P])
        mx = sb("mx", [P, H])
        ov = ring("ov", 2, [P, NG, P])
        rden = sb("rden", [P, H, 1])
        on = ring("on", 2, [P, D])
        at = ring("at", 2, [P, KC, P])
        st1, st2 = sb("st1", [P, 6]), sb("st2", [P, 6])
        mv = sb("mv", [P, 2, 2])
        std = sb("std", [P, 2])
        rstd = sb("rstd", [P, 2])
        attention_region.close()
        region[0] = ctx
        IP = IC * P
        wgi = sb("wgi", [P, KC, IP], bf16)
        wui = sb("wui", [P, KC, IP], bf16)
        wdi = sb("wdi", [P, IC, D], bf16)
        wq_b = sb("wq_b", [P, KC * IP], bf16)
        s_gu = sb("s_gu", [P, 2, IC])
        s_gux = sb("s_gux", [P, 2, IC])
        s_d = sb("s_d", [P, KC])
        inv = sb("inv", [P, 4 * IC])
        sd_row = sb("sd_row", [P, D])
        xq_f = ring("xq_f", 2, [P, TPC * D])
        xq_b = ring("xq_b", 2, [P, TPC, D], bf16)
        W_BYTES = 4 * (2 * IC * D + KC * I)
        xqt_all = sb("xqt", [P, max(KC * T, W_BYTES // 2)], bf16)
        xqt = xqt_all[:, 0:KC * T].rearrange("p (k t) -> p k t", k=KC)
        raw = xqt_all[:, 0:W_BYTES // 2].bitcast(f32)
        f_sg = ring("f_sg", 3, [P, CT])
        f_h = ring("f_h", 3, [P, CT])
        f_q = [big[:, n * IC * CT // 2:(n + 1) * IC * CT // 2].bitcast(bf16).rearrange("p (c t) -> p c t", c=IC) for n in range(2)]
        yo = ring("yo", 2, [P, D])
        yo2 = ring("yo2", 4, [P, D])
        wraw = [raw[:, n * IC * D:(n + 1) * IC * D].rearrange("p (c d) -> p c d", c=IC) for n in range(2)]
        wdraw = raw[:, 2 * IC * D:2 * IC * D + KC * I].rearrange("p (k i) -> p k i", k=KC)

        def phase_end(eng, n):
            eng.drain().then_inc(sem("phase_done"), 1)
            eng.wait_ge(sem("phase_done"), 5 * n)

        def wait(eng, name, value):
            if not (isinstance(value, int) and value <= 0):
                eng.wait_ge(sem(name), value)

        def hold(eng):
            eng.sem_inc(sem("held"), 1)

        def ahead(b, n):
            return min(b + n, NB) if isinstance(b, int) else b + n

        class Steps:

            def __init__(self, eng, name, n, b):
                self.eng, self.name, self.n, self.b, self.k = eng, name, n, b, 0

            def then(self, ins):
                self.k += 1
                assert self.k <= self.n, self.name
                ins.then_inc(sem(self.name), 1)
                self.eng.wait_ge(sem(self.name), self.b * self.n + self.k)

            def end(self):
                assert self.k == self.n, (self.name, self.k)

        def slots(eng, body, nb, slot0, loop_end, first, last, unroll):
            def at_slot(s):
                def stage(lag):
                    b = s - lag
                    return (b, b % 4) if 0 <= b < nb else None
                body(stage)
            for s in range(first, min(slot0, last)):
                at_slot(s)
            if loop_end > slot0:
                assert (loop_end - slot0) % unroll == 0
                with eng.Fori(slot0, loop_end - unroll + 1, unroll) as i:
                    for u in range(unroll):
                        body(lambda lag, u=u: (i + (u - lag), (slot0 + u - lag) % 4))
            for s in range(max(loop_end, slot0), last):
                at_slot(s)

        def attention_slots(eng, body):
            slots(eng, body, NB, SLOT0, LOOP_END, -1, NB + LAGS, UNROLL)


        def attention_pe(pe, L):
            def sm(name):
                return f"{name}_{L}"

            def scores(m, g):
                if m is None:
                    return
                b, r = m
                p, j = r % 2, g // (NG // KC)
                if g == 0:
                    wait(pe, sm(f"kbd_in{p}"), 64 * (b - p) + 128)
                bk = bank[g % 2]
                wait(pe, sm("sub_done"), 4 * b + g - 1)
                if L == 1:
                    nc.tensor.matmul(bk[:, :], identb[:, :], mask_bias[:, :].unsqueeze(1).broadcast_to([P, GH, S]),
                                     start=True, stop=False)
                c0 = (g % (NG // KC)) * GH * P
                nc.tensor.matmul(bk[:, :], qk[p][:, j, :], kbd[p][:, j, c0:c0 + GH * P],
                                 start=(L == 0), stop=True).then_inc(sem(sm("s_done")), 1)

            def probs_t(m, g):
                if m is None:
                    return
                b, _ = m
                wait(pe, sm("exp_done"), 4 * b + g + 1)
                wait(pe, sm("pt_out"), 4 * b + g - 1)
                for h in range(GH):
                    last = nc.tensor.transpose(bank[2 + g % 2][:, h * P:(h + 1) * P], sc[g][:, h, :], ident[:, :])
                last.then_inc(sem(sm("pt_done")), 1)

            def values(m, g):
                if m is None:
                    return
                b, r = m
                p = r % 2
                wait(pe, sm("pt_out"), 4 * b + g + 1)
                if g == 0:
                    wait(pe, sm("v_out"), b + 1)
                    wait(pe, sm("ov_out"), b)
                for h in range(GH):
                    last = nc.tensor.matmul(bank[7][32 * h:32 * h + 32, g * P:(g + 1) * P], vx[p][:, GH * g + h, :],
                                            pt[g % 2][:, h, :], start=True, stop=True)
                last.then_inc(sem(sm("pv_done")), 1)

            def transposes(f):
                if f is None:
                    return
                b, r = f
                p = r % 2
                wait(pe, sm("xn1_done"), b + 1)
                wait(pe, sm(f"cx_in{p}"), 8 * (b - p) + 16)
                wait(pe, sm("at_out"), b - 2)
                if L == 0:
                    wait(pe, sm("en_out"), b - 3)
                for c in range(2 * KC):
                    src = (xn if c < KC else cx)[p][:, (c % KC) * P:(c % KC + 1) * P]
                    last = nc.tensor.transpose(bank[4][:, c * P:(c + 1) * P], src, ident[:, :])
                last.then_inc(sem(sm("t_done")), 1)

            def project_qk(f):
                if f is None:
                    return
                b, r = f
                p = r % 2
                wait(pe, sm("xt_out"), b + 1)
                if L == 0:
                    wait(pe, sm("silu_done"), b - 3)
                else:
                    wait(pe, sm("qk_out"), b)
                for n, w in enumerate((w_q, w_k)):
                    for j in range(KC):
                        for c in range(KC):
                            last = nc.tensor.matmul(bank[5][:, (n * KC + j) * P:(n * KC + j + 1) * P],
                                                    w[:, c, j * P:(j + 1) * P], xt[p][:, n * KC + c, :],
                                                    start=(c == 0), stop=(c == KC - 1))
                last.then_inc(sem(sm("qk_done")), 1)

            def project_v(f):
                if f is None:
                    return
                b, r = f
                p = r % 2
                wait(pe, sm("x3_done"), b - 2)
                if L == 0:
                    wait(pe, sm("pos_done"), b - 4)
                for c in range(KC):
                    last = nc.tensor.matmul(bank[6][:, 0:D], xt[p][:, KC + c, :], w_v[:, c, :],
                                            start=(c == 0), stop=(c == KC - 1))
                last.then_inc(sem(sm("v_done")), 1)

            def output(k):
                if k is None:
                    return
                b, r = k
                wait(pe, sm("at_out"), b + 1)
                wait(pe, sm("v_out"), ahead(b, 3))
                if L == 0:
                    wait(pe, sm("pos_done"), b - 1)
                for c in range(KC):
                    last = nc.tensor.matmul(bank[6][:, 0:D], at[r % 2][:, c, :], w_o[:, c, :],
                                            start=(c == 0), stop=(c == KC - 1))
                last.then_inc(sem(sm("o_done")), 1)

            def heads_to_tokens(k):
                if k is None:
                    return
                b, r = k
                wait(pe, sm("ov_out"), b + 1)
                wait(pe, sm("xt_out"), ahead(b, 3))
                if L == 0:
                    wait(pe, sm("xa_done"), b - 1)
                for g in range(NG):
                    last = nc.tensor.transpose(bank[4][:, g * P:(g + 1) * P], ov[r % 2][:, g, :], ident[:, :])
                last.then_inc(sem(sm("ot_done")), 1)

            def tokens_to_heads(k):
                if k is None:
                    return
                b, r = k
                wait(pe, sm("on_done"), b + 1)
                for c in range(KC):
                    last = nc.tensor.transpose(bank[4][:, c * P:(c + 1) * P], on[r % 2][:, c * P:(c + 1) * P], ident[:, :])
                last.then_inc(sem(sm("at_done")), 1)

            def moe_transposes(k):
                if k is None:
                    return
                b, r = k
                wait(pe, sm("xn2_done"), b + 1)
                wait(pe, sm("qk_out"), ahead(b, 4))
                wait(pe, sm("silu_done"), b)
                for c in range(KC):
                    last = nc.tensor.transpose(bank[5][:, c * P:(c + 1) * P], pay[r][:, c * P:(c + 1) * P], ident[:, :])
                last.then_inc(sem(sm("t2_done")), 1)

            def moe_up(k):
                if k is None:
                    return
                b, r = k
                p = r % 2
                wait(pe, sm("x2t_out"), b + 1)
                for n, w in enumerate((w_sg, w_su)):
                    for j in range(FS // P):
                        for c in range(KC):
                            last = nc.tensor.matmul(bank[5][:, n * FS + j * P:n * FS + (j + 1) * P],
                                                    w[:, c, j * P:(j + 1) * P], x2t[p][:, c, :],
                                                    start=(c == 0), stop=(c == KC - 1))
                last.then_inc(sem(sm("up_done")), 1)
                wait(pe, sm("at_out"), ahead(b, 2))
                for c in range(KC):
                    last = nc.tensor.matmul(bank[4][:, 256:256 + E], x2t[p][:, c, :], w_gate[:, c, :],
                                            start=(c == 0), stop=(c == KC - 1))
                last.then_inc(sem(sm("logits_done")), 1)

            def moe_down(k):
                if k is None:
                    return
                b, r = k
                wait(pe, sm("silu_done"), b + 1)
                wait(pe, sm("xt_out"), ahead(b, 5))
                wait(pe, sm("en_out"), b + 1)
                wait(pe, sm("at_out"), ahead(b, 2))
                for c in range(FS // P):
                    last = nc.tensor.matmul(bank[4][:, 0:D], ht[r % 2][:, c, :], w_sd[:, c, :],
                                            start=(c == 0), stop=(c == FS // P - 1))
                last.then_inc(sem(sm("down_done")), 1)

            def moe_counts(k):
                if k is None:
                    return
                b, r = k
                wait(pe, sm("sel_done"), b + 1)
                wait(pe, sm("x3_done"), ahead(b, 2))
                wait(pe, sm("v_out"), ahead(b, 4))
                nc.tensor.matmul(bank[6][:, D:D + E], strict_tri[:, :], sel[r % 2][:, :], start=True, stop=True)
                nc.tensor.matmul(bank[6][:, D + E:D + 2 * E], onesb[:, :], sel[r % 2][:, :], start=True,
                                 stop=True).then_inc(sem(sm("counts_done")), 1)

            def body(stage):
                f, m, k, o, w = stage(0), stage(1), stage(2), stage(3), stage(4)
                scores(m, 0)
                transposes(f)
                output(o)
                probs_t(k, 3)
                values(k, 2)
                scores(m, 1)
                project_qk(f)
                if L == 0:
                    moe_down(w)
                probs_t(m, 0)
                values(k, 3)
                scores(m, 2)
                if L == 0:
                    moe_counts(w)
                project_v(f)
                if L == 0:
                    moe_transposes(o)
                heads_to_tokens(k)
                probs_t(m, 1)
                values(m, 0)
                scores(m, 3)
                tokens_to_heads(k)
                if L == 0:
                    moe_up(o)
                probs_t(m, 2)
                values(m, 1)

            attention_slots(pe, body)

        def attention_act(act, L):
            def sm(name):
                return f"{name}_{L}"

            def exponent(m, g):
                if m is None:
                    return
                b, _ = m
                wait(act, sm("sub_done"), 4 * b + g + 1)
                nc.scalar.activation(sc[g][:, :, :], sc[g][:, :, :], ACT.Exp, scale=SM_SCALE).then_inc(sem(sm("exp_done")), 1)

            def copy_pt(m, g):
                if m is None:
                    return
                b, _ = m
                wait(act, sm("pt_done"), 4 * b + g + 1)
                wait(act, sm("pv_done"), 4 * b + g - 1)
                nc.scalar.copy(pt[g % 2][:, :, :], bank[2 + g % 2][:, :].rearrange("p (h q) -> p h q", h=GH)
                               ).then_inc(sem(sm("pt_out")), 1)

            def copy_xt(f):
                if f is None:
                    return
                b, r = f
                wait(act, sm("t_done"), b + 1)
                wait(act, sm("v_done"), b - 1)
                nc.scalar.copy(xt[r % 2][:, :, :], bank[4][:, :].rearrange("p (c t) -> p c t", c=2 * KC)
                               ).then_inc(sem(sm("xt_out")), 1)

            def copy_ov(k):
                if k is None:
                    return
                b, r = k
                wait(act, sm("pv_done"), 4 * b + 4)
                wait(act, sm("ot_done"), b - 1)
                nc.scalar.copy(ov[r % 2][:, :, :], bank[7][:, :].rearrange("p (g q) -> p g q", g=NG)
                               ).then_inc(sem(sm("ov_out")), 1)

            def copy_at(k):
                if k is None:
                    return
                b, r = k
                wait(act, sm("at_done"), b + 1)
                wait(act, sm("o_done"), b - 1)
                nc.scalar.copy(at[r % 2][:, :, :], bank[4][:, 0:D].rearrange("p (c t) -> p c t", c=KC)
                               ).then_inc(sem(sm("at_out")), 1)

            def copy_x2t(k):
                if k is None:
                    return
                b, r = k
                wait(act, sm("t2_done"), b + 1)
                wait(act, sm("up_done"), b - 1)
                nc.scalar.copy(x2t[r % 2][:, :, :], bank[5][:, 0:D].rearrange("p (c t) -> p c t", c=KC)
                               ).then_inc(sem(sm("x2t_out")), 1)

            def moe_functions(k):
                if k is None:
                    return
                b, r = k
                p = r % 2
                wait(act, sm("up_done"), b + 1)
                wait(act, sm("silu_done"), b - 1)
                nc.scalar.activation(th[p][:, :], bank[5][:, 0:FS], ACT.Tanh, scale=0.5).then_inc(sem(sm("th_out")), 1)
                wait(act, sm("logits_done"), b + 1)
                wait(act, sm("sel_done"), b - 1)
                nc.scalar.activation(en[p][:, :], bank[4][:, 256:256 + E], ACT.Exp, scale=-1.0).then_inc(sem(sm("en_out")), 1)

            def deviations(n, stage):
                wait(act, sm("stats_done"), n)
                nc.scalar.activation(std[:, :], mv[:, :, 1], ACT.Sqrt, bias=eps_col[:, 0:1]).then_inc(sem(sm("std_done")), 1)

            def body(stage):
                f, m, k, o = stage(0), stage(1), stage(2), stage(3)
                copy_xt(f)
                exponent(m, 0)
                copy_pt(k, 3)
                if stage(-1) is not None or o is not None:
                    s1 = stage(-1)[0] if stage(-1) is not None else o[0] + 4
                    deviations(s1 + 1, stage)
                exponent(m, 1)
                copy_pt(m, 0)
                copy_ov(k)
                exponent(m, 2)
                if L == 0:
                    copy_x2t(o)
                copy_pt(m, 1)
                exponent(m, 3)
                copy_at(k)
                if L == 0:
                    moe_functions(o)
                copy_pt(m, 2)

            attention_slots(act, body)

        def attention_dve(dve, L):
            def sm(name):
                return f"{name}_{L}"

            def row(b):
                return res[:, bass.ds(b, 1), :].rearrange("p o d -> p (o d)")

            def maxima(m, g):
                if m is None:
                    return
                b, _ = m
                wait(dve, sm("s_done"), 4 * b + g + 1)
                st = Steps(dve, sm("max_step"), 4, b)
                st.k = g
                bk = bank[g % 2][:, :].rearrange("p (h k) -> p h k", h=GH)
                st.then(nc.vector.tensor_reduce(mx[:, GH * g:GH * g + GH], bk, AX, ALU.max))
                wait(dve, sm("pt_done"), 4 * b + g - 3)
                nc.vector.tensor_tensor(sc[g][:, :, :], bk,
                                        mx[:, GH * g:GH * g + GH].unsqueeze(2).broadcast_to([P, GH, S]),
                                        ALU.subtract).then_inc(sem(sm("sub_done")), 1)

            def residual(k):
                if k is None:
                    return
                b, _ = k
                st = Steps(dve, sm("res_step"), 3, b)
                wait(dve, sm("o_done"), b + 1)
                st.then(nc.vector.scalar_tensor_tensor(row(b), bank[6][:, 0:D], tg[:, L:L + 1], row(b), ALU.mult, ALU.add))
                st.then(nc.vector.tensor_tensor(row(b), row(b), o_bias[:, :], ALU.add))
                dve.sem_inc(sem(sm("x3_done")), 1)
                hold(dve)
                st.then(nc.vector.bn_stats(st2[:, :], row(b)))
                st.end()

            def first_stats(n):
                if n is None:
                    return
                b, r = n
                p = r % 2
                if L == 0:
                    wait(dve, f"res_in{r}", 4 * (b - r) + 16)
                    nst = 1
                else:
                    nst = 2
                st = Steps(dve, sm("ln1_step"), nst, b)
                if L == 1:
                    wait(dve, f"ax_in{p}", 16 * (b - p) + 32)
                    st.then(nc.vector.tensor_tensor(row(b), ax[p][:, 0, :], ax[p][:, 1, :], ALU.add))
                hold(dve)
                st.then(nc.vector.bn_stats(st1[:, :], row(b)))
                st.end()

            def variances(n, k):
                last = None
                hold(dve)
                if n is not None:
                    last = nc.vector.bn_aggr(mv[:, 0, :], st1[:, :])
                if k is not None:
                    last = nc.vector.bn_aggr(mv[:, 1, :], st2[:, :])
                if last is not None:
                    last.then_inc(sem(sm("stats_done")), 1)

            def normalise(n, k):
                if n is None and k is None:
                    return
                s1 = n[0] if n is not None else k[0] + 4
                wait(dve, sm("std_done"), s1 + 1)
                st = Steps(dve, sm("rstd_step"), 1, s1)
                st.then(nc.vector.reciprocal(rstd[:, :], std[:, :]))
                if n is not None:
                    b, r = n
                    wait(dve, sm("t_done"), b - 1)
                    nc.vector.tensor_scalar(xn[r % 2][:, :], row(b), mv[:, 0, 0:1], rstd[:, 0:1], ALU.subtract,
                                            ALU.mult).then_inc(sem(sm("xn1_done")), 1)
                if k is not None:
                    b, r = k
                    if L == 0:
                        wait(dve, f"scattered{r}", 32 * (b - r))
                        dst = pay[r][:, 0:D]
                    else:
                        dst = xn3[:, bass.ds(b, 1), :].rearrange("p o d -> p (o d)")
                    nc.vector.tensor_scalar(dst, row(b), mv[:, 1, 0:1], rstd[:, 1:2], ALU.subtract,
                                            ALU.mult).then_inc(sem(sm("xn2_done")), 1)

            def bias_qk(f):
                if f is None:
                    return
                b, r = f
                p = r % 2
                wait(dve, sm("qk_done"), b + 1)
                wait(dve, sm("s_done"), 4 * (b - 1))
                wait(dve, sm(f"kbd_in{p}"), 64 * (b - p))
                nc.vector.tensor_tensor(qk[p][:, :, :], bank[5][:, :].rearrange("p (c t) -> p c t", c=2 * KC),
                                        qk_bias[:, :].unsqueeze(2).broadcast_to([P, 2 * KC, P]),
                                        ALU.add).then_inc(sem(sm("qk_out")), 1)

            def bias_v(f):
                if f is None:
                    return
                b, r = f
                wait(dve, sm("v_done"), b + 1)
                wait(dve, sm("pv_done"), 4 * (b - 1))
                nc.vector.tensor_tensor(vx[r % 2][:, :, 0:DH], bank[6][:, 0:D].rearrange("p (h d) -> p h d", h=H),
                                        v_bias[:, :].rearrange("p (h d) -> p h d", h=H),
                                        ALU.add).then_inc(sem(sm("v_out")), 1)

            def head_norm(k):
                if k is None:
                    return
                b, r = k
                wait(dve, sm("ot_done"), b + 1)
                wait(dve, sm("at_done"), b - 1)
                st = Steps(dve, sm("norm_step"), 1, b)
                o = bank[4][:, :].rearrange("p (h e) -> p h e", e=32)
                st.then(nc.vector.reciprocal(rden[:, :, :], o[:, :, DH:DH + 1]))
                nc.vector.tensor_tensor(on[r % 2][:, :].rearrange("p (h d) -> p h d", h=H), o[:, :, 0:DH],
                                        rden[:, :, :].broadcast_to([P, H, DH]), ALU.mult).then_inc(sem(sm("on_done")), 1)
                st.end()

            def silu(k):
                if k is None:
                    return
                b, r = k
                wait(dve, sm("th_out"), b + 1)
                wait(dve, sm("down_done"), b - 1)
                st = Steps(dve, sm("silu_step"), 1, b)
                st.then(nc.vector.scalar_tensor_tensor(hs[:, :], th[r % 2][:, :], 1.0, bank[5][:, 0:FS], ALU.add, ALU.mult))
                nc.vector.tensor_tensor(ht[r % 2][:, :, :].rearrange("p c t -> p (c t)"), hs[:, :], bank[5][:, FS:2 * FS],
                                        ALU.mult).then_inc(sem(sm("silu_done")), 1)
                st.end()

            def shared_out(k):
                if k is None:
                    return
                b, r = k
                p = r % 2
                wait(dve, sm("down_done"), b + 1)
                wait(dve, f"xa_stored{p}", 8 * (b - p))
                nc.vector.scalar_tensor_tensor(xa[p][:, :], bank[4][:, 0:D], tg_half[:, 0:1], row(b), ALU.mult,
                                               ALU.add).then_inc(sem(sm("xa_done")), 1)

            def route(k):
                if k is None:
                    return
                b, r = k
                st = Steps(dve, sm("route_step"), 16, b)
                V = nc.vector
                wait(dve, sm("en_out"), b + 1)
                st.then(V.tensor_scalar(score[:, :], en[r % 2][:, :], 1.0, None, ALU.add))
                st.then(V.reciprocal(score[:, :], score[:, :]))
                st.then(V.tensor_tensor(sfc[:, :], score[:, :], ebias[:, :], ALU.add))
                hold(dve)
                for g in range(EG):
                    last = V.max(m8[:, g, :], sfc[:, g * EPG:(g + 1) * EPG])
                st.then(last)
                st.then(V.tensor_tensor(gs[:, 0:EG], m8[:, :, 0], m8[:, :, 1], ALU.add))
                hold(dve)
                st.then(V.max(top[:, :], gs[:, 0:EG]))
                st.then(V.tensor_copy(tog[:, 0:GSEL], top[:, 0:GSEL]))
                hold(dve)
                st.then(V.match_replace(grep[:, :], tog[:, :], gs[:, :], -LOW))
                st.then(V.tensor_scalar(gmask[:, :, 0], grep[:, 0:EG], -LOW, None, ALU.is_ge))
                st.then(V.tensor_tensor(tmp[:, :].rearrange("p (g e) -> p g e", g=EG),
                                        sfc[:, :].rearrange("p (g e) -> p g e", g=EG),
                                        gmask[:, :, :].broadcast_to([P, EG, EPG]), ALU.mult))
                st.then(V.tensor_scalar(tmp[:, :], tmp[:, :], 0.0, None, ALU.add))
                hold(dve)
                st.then(V.max(top[:, :], tmp[:, :]))
                hold(dve)
                st.then(V.match_replace(rep[:, :], top[:, :], tmp[:, :], LOW))
                wait(dve, sm("counts_done"), b - 1)
                V.tensor_scalar(sel[r % 2][:, :], rep[:, :], LOW, None, ALU.is_le).then_inc(sem(sm("sel_done")), 1)
                V.tensor_scalar(self_[:, :], rep[:, :], LOW, None, ALU.is_le)
                st.then(V.scalar_tensor_tensor(wun[:, :], rep[:, :], LOW, score[:, :], ALU.is_le, ALU.mult,
                                               accum_out=wsum[:, 0:1]))
                st.then(V.tensor_scalar(wsum[:, :], wsum[:, :], 1e-20, None, ALU.add))
                st.then(V.reciprocal(wsum[:, :], wsum[:, :]))
                V.tensor_scalar(pay[r][:, D:D + E], wun[:, :], wsum[:, 0:1], tg_route[:, 0:1], ALU.mult, ALU.mult)
                V.tensor_scalar(pay[r][:, TOKC:TOKC + 1], pay[r][:, TOKC:TOKC + 1], 4.0 * P, None, ALU.add)
                st.end()

            def dispatch(k):
                if k is None:
                    return
                b, r = k
                st = Steps(dve, sm("slot_step"), 6, b)
                V = nc.vector
                wait(dve, sm("counts_done"), b + 1)
                st.then(V.tensor_tensor(pos[:, :], bank[6][:, D:D + E], count[:, :], ALU.add))
                V.tensor_tensor(count[:, :], bank[6][:, D + E:D + 2 * E], count[:, :], ALU.add).then_inc(sem(sm("pos_done")), 1)
                V.tensor_tensor(key[:, :], pos[:, :], slot_base[:, :], ALU.add)
                st.then(V.scalar_tensor_tensor(valid[:, :], pos[:, :], float(CAP), self_[:, :], ALU.is_lt, ALU.mult))
                st.then(V.tensor_tensor(key[:, :], key[:, :], valid[:, :], ALU.mult))
                hold(dve)
                st.then(V.max(keys8[:, :], key[:, :]))
                st.then(V.tensor_scalar(far[:, :], keys8[:, :], 0.0, float(1 << 20), ALU.is_equal, ALU.mult))
                st.then(V.scalar_tensor_tensor(idx[r][:, :], keys8[:, :], -1.0, far[:, :], ALU.add, ALU.add))
                dve.sem_inc(sem(sm("idx_done")), 1)
                st.end()

            def body(stage):
                n, f, m, k, o, w = stage(-1), stage(0), stage(1), stage(2), stage(3), stage(4)
                maxima(m, 0)
                if L == 0:
                    silu(w)
                residual(o)
                first_stats(n)
                variances(n, o)
                maxima(m, 1)
                bias_qk(f)
                normalise(n, o)
                if L == 0:
                    shared_out(w)
                    route(w)
                maxima(m, 2)
                bias_v(f)
                head_norm(k)
                maxima(m, 3)
                if L == 0:
                    dispatch(w)

            attention_slots(dve, body)

        def attention_sp(sp, L):
            def sm(name):
                return f"{name}_{L}"

            ctx_v = a["ctx_1024"]

            def load(n):
                if n is None:
                    return
                b, r = n
                p = r % 2
                wait(sp, sm("t_done"), b - 1)
                hold(sp)
                sp.dma_start(cx[p][:, :], ctx_v[bass.ds(b, 1), :, :].rearrange("o p d -> p (o d)")
                             ).then_inc(sem(sm(f"cx_in{p}")), 16)
                if L == 0:
                    sp.dma_start(res[:, bass.ds(b, 1), :].rearrange("p o d -> p (o d)"),
                                 a["x"][bass.ds(b, 1), :, :].rearrange("o p d -> p (o d)")).then_inc(sem(f"res_in{r}"), 16)
                else:
                    wait(sp, sm("ln1_step"), 2 * (b - 1))
                    hold(sp)
                    for n_ in range(2):
                        sp.dma_start(ax[p][:, n_, :], acc[n_][bass.ds(b * P, P), :]).then_inc(sem(f"ax_in{p}"), 16)

            def spread(f):
                if f is None:
                    return
                b, r = f
                p = r % 2
                wait(sp, sm("qk_out"), b + 1)
                hold(sp)
                for h in range(HB):
                    sp.dma_start(kbd[p][DH * h:DH * (h + 1), :, h * P:(h + 1) * P],
                                 qk[p][DH * h:DH * (h + 1), KC:2 * KC, :]).then_inc(sem(sm(f"kbd_in{p}")), 16)

            def store(k):
                if k is None:
                    return
                b, r = k
                wait(sp, sm("xa_done"), b + 1)
                hold(sp)
                sp.dma_start(acc[0][bass.ds(b * P, P), :], xa[r % 2][:, :]).then_inc(sem(f"xa_stored{r % 2}"), 16)

            def body(stage):
                load(stage(-2))
                spread(stage(0))
                if L == 0:
                    store(stage(4))

            load((0, 0))
            attention_slots(sp, body)

        def expert_slots(eng, body):
            slots(eng, body, E, 4, 4 + (E - 4) // 4 * 4, 0, E + 2, 4)

        def experts_sp(sp):
            xe_v = xe.rearrange("(e h p) c -> e p h c", p=P, h=HALVES)

            def load(e):
                if e is None:
                    return
                b, r = e
                p = r % 2
                wait(sp, "e_up_done", b - 1)
                wait(sp, "e_down_done", b - 1)
                wait(sp, "e_w_done", b - 1)
                hold(sp)
                one = bass.ds(b, 1)
                sp.dma_start(xr[p][:, :, :], xe_v[one].rearrange("o p h c -> p (o h) c")).then_inc(sem(f"e_in{p}"), 16)
                sp.dma_start(wa[p][:, :, :], a["L0_ffn_w1"][one].rearrange("o (k p) f -> p (o k) f", p=P)).then_inc(sem(f"e_in{p}"), 16)
                sp.dma_start(wb[p][:, :, :], a["L0_ffn_w3"][one].rearrange("o (k p) f -> p (o k) f", p=P)).then_inc(sem(f"e_in{p}"), 16)
                sp.dma_start(wc[p][:, :], a["L0_ffn_w2"][one].rearrange("o f d -> f (o d)")).then_inc(sem(f"e_in{p}"), 16)

            expert_slots(sp, lambda stage: load(stage(0)))

        def experts_pe(pe):
            def rows_t(e):
                if e is None:
                    return
                b, r = e
                p = r % 2
                wait(pe, f"e_in{p}", 32 * (b - p) + 64)
                wait(pe, "e_xt_out", b - 1)
                for c in range(KC):
                    for h in range(HALVES):
                        last = nc.tensor.transpose(bank[p][:, c * CAP + h * P:c * CAP + (h + 1) * P],
                                                   xr[p][:, h, c * P:(c + 1) * P], ident[:, :])
                last.then_inc(sem("e_t_done"), 1)

            def up(e):
                if e is None:
                    return
                b, r = e
                p = r % 2
                wait(pe, "e_xt_out", b + 1)
                wait(pe, "e_h_done", b - 1)
                for n, w in enumerate((wa, wb)):
                    for c in range(KC):
                        last = nc.tensor.matmul(bank[2 + p][:, n * CAP:(n + 1) * CAP], w[p][:, c, :], xrt[p][:, c, :],
                                                start=(c == 0), stop=(c == KC - 1))
                last.then_inc(sem("e_up_done"), 1)

            def down(e):
                if e is None:
                    return
                b, r = e
                p = r % 2
                wait(pe, "e_h_done", b + 1)
                wait(pe, "e_y_done", b - 1)
                for h in range(HALVES):
                    last = nc.tensor.matmul(bank[4 + p][:, h * D:(h + 1) * D], he[p][:, h * P:(h + 1) * P], wc[p][:, :],
                                            start=True, stop=True)
                last.then_inc(sem("e_down_done"), 1)

            def body(stage):
                rows_t(stage(0))
                down(stage(1))
                up(stage(0))

            expert_slots(pe, body)

        def experts_act(act):
            def copy_t(e):
                if e is None:
                    return
                b, r = e
                wait(act, "e_t_done", b + 1)
                wait(act, "e_up_done", b - 1)
                nc.scalar.copy(xrt[r % 2][:, :, :], bank[r % 2][:, :].rearrange("p (c t) -> p c t", c=KC)).then_inc(sem("e_xt_out"), 1)

            def silu(e):
                if e is None:
                    return
                b, r = e
                wait(act, "e_up_done", b + 1)
                wait(act, "e_h_done", b - 1)
                nc.scalar.activation(sg[r % 2][:, :], bank[2 + r % 2][:, 0:CAP], ACT.Silu).then_inc(sem("e_sg_done"), 1)

            def body(stage):
                copy_t(stage(0))
                silu(stage(0))

            expert_slots(act, body)

        def experts_dve(dve):
            def weights(e):
                if e is None:
                    return
                b, r = e
                p = r % 2
                wait(dve, f"e_in{p}", 32 * (b - p) + 64)
                wait(dve, "e_y_done", b - 1)
                wait(dve, f"e_added{p}", 16 * (b - p))
                nc.vector.tensor_copy(wcol[p][:, :].unsqueeze(2), xr[p][:, :, bass.ds(b + D, 1)])
                nc.vector.tensor_copy(tid[p][:, :], xr[p][:, :, TOKC]).then_inc(sem("e_w_done"), 1)

            def hidden(e):
                if e is None:
                    return
                b, r = e
                p = r % 2
                wait(dve, "e_sg_done", b + 1)
                wait(dve, "e_down_done", b - 1)
                nc.vector.tensor_tensor(he[p][:, :], sg[p][:, :], bank[2 + p][:, CAP:2 * CAP], ALU.mult).then_inc(sem("e_h_done"), 1)

            def outputs(e):
                if e is None:
                    return
                b, r = e
                p = r % 2
                wait(dve, "e_down_done", b + 1)
                wait(dve, "e_w_done", b + 1)
                for h in range(HALVES):
                    last = nc.vector.tensor_scalar(ye[p][:, h, :], bank[4 + p][:, h * D:(h + 1) * D], wcol[p][:, h:h + 1], None, ALU.mult)
                last.then_inc(sem("e_y_done"), 1)

            def body(stage):
                weights(stage(0))
                outputs(stage(1))
                hidden(stage(0))

            expert_slots(dve, body)

        def experts_pool(pool):
            def add(e):
                if e is None:
                    return
                b, r = e
                p = r % 2
                wait(pool, "e_y_done", b + 1)
                wait(pool, f"e_added{p}", 16 * (b - p))
                hold(pool)
                for h in range(HALVES):
                    nc.gpsimd.indirect_dma_start(
                        out=acc[p][:, :], out_offset=bass.IndirectOffsetOnAxis(ap=tid[p][:, h:h + 1], axis=0),
                        in_=ye[p][:, h, :], in_offset=None, bounds_check=T + HALVES * P - 1, oob_is_err=True,
                        compute_op=ALU.add).then_inc(sem(f"e_added{p}"), 16)

            expert_slots(pool, lambda stage: add(stage(1)))
            for p in range(2):
                pool.wait_ge(sem(f"e_added{p}"), 16 * E)

        GUB = 3

        def weights_dve(dve):
            V = nc.vector
            st = Steps(dve, "wq_step", 8 * 2 + 8, 0)
            dve.wait_ge(sem("ffn_w_in"), 16 * (5 if IREST else 3))
            for n in range(2):
                st.then(V.tensor_reduce(s_gu[:, n, 0:IC], wraw[n], AX, ALU.max, apply_absolute_value=True))
                st.then(V.tensor_scalar(s_gu[:, n, :], s_gu[:, n, :], 1.0 / QMAX, None, ALU.mult))
                if IREST:
                    st.then(V.tensor_scalar(inv[:, 0:1], s_gu[:, n, 0:1], 1.0, None, ALU.mult))
                    st.then(V.memset(s_gu[IREST:P, n, IC - 1:IC], 1.0))
                st.then(V.reciprocal(inv[:, n * IC:(n + 1) * IC], s_gu[:, n, :]))
                st.then(V.tensor_tensor(wraw[n], wraw[n], inv[:, n * IC:(n + 1) * IC].unsqueeze(2).broadcast_to([P, IC, D]), ALU.mult))
                st.then(V.tensor_scalar(wraw[n], wraw[n], RND, -RND, ALU.add, ALU.add))
                if n == 1:
                    dve.wait_ge(sem("w_t_out"), 1)
                st.then(V.tensor_scalar(wq_b[:, 0:IC * D].rearrange("p (c d) -> p c d", c=IC), wraw[n], QMAX, -QMAX - 1.0, ALU.min, ALU.max))
                dve.sem_inc(sem("w_int"), 1)
            st.then(V.tensor_reduce(s_d[:, :], wdraw[:, :, :], AX, ALU.max, apply_absolute_value=True))
            st.then(V.tensor_scalar(s_d[:, :], s_d[:, :], 1.0 / QMAX, None, ALU.mult))
            st.then(V.reciprocal(inv[:, 2 * IC:2 * IC + KC], s_d[:, :]))
            st.then(V.tensor_tensor(wdraw[:, :, :], wdraw[:, :, :], inv[:, 2 * IC:2 * IC + KC].unsqueeze(2).broadcast_to([P, KC, I]), ALU.mult))
            st.then(V.tensor_scalar(wdraw[:, :, :], wdraw[:, :, :], RND, -RND, ALU.add, ALU.add))
            dve.wait_ge(sem("w_t_out"), 2)
            wd_b = wq_b[:, :].rearrange("p (c i) -> p c i", c=KC)
            st.then(V.memset(wd_b[:, :, I:IP], 0.0)) if IP > I else st.then(V.memset(inv[:, 0:1], 0.0))
            st.then(V.tensor_scalar(wd_b[:, :, 0:I], wdraw[:, :, :], QMAX, -QMAX - 1.0, ALU.min, ALU.max))
            dve.sem_inc(sem("w_int"), 1)
            dve.wait_ge(sem("gmax_done"), 1)
            dve.wait_ge(sem("sig_done"), 1)
            st.then(V.tensor_scalar(sig[:, :], sig[:, :], 1.0, None, ALU.add))
            st.end()
            st = Steps(dve, "sx_step", 4, 0)
            st.then(V.reciprocal(sig[:, :], sig[:, :]))
            st.then(V.tensor_scalar(scl[:, 0:1], gmax[:, 0:1], sig[:, 0:1], 1.0 / QMAX, ALU.mult, ALU.mult))
            st.then(V.reciprocal(scl[:, 1:2], scl[:, 0:1]))
            st.then(V.tensor_scalar(s_gux[:, :, :], s_gu[:, :, :], scl[:, 0:1], None, ALU.mult))
            dve.sem_inc(sem("sx_done"), 1)
            st.end()

        def weights_pe(pe):
            bb = [bank[k][:, :].bitcast(bf16) for k in range(3)]
            for n in range(3):
                pe.wait_ge(sem("w_int"), n + 1)
                for half in range(2):
                    if n or half:
                        pe.wait_ge(sem("w_half_out"), 2 * n + half)
                    for c in range(IC):
                        if n < 2:
                            src = wq_b[:, c * D + half * P:c * D + (half + 1) * P]
                        else:
                            src = wq_b[:, half * IP + c * P:half * IP + (c + 1) * P]
                        last = nc.tensor.transpose(bb[0][:, c * P:(c + 1) * P], src, identb[:, :])
                    last.then_inc(sem("w_half_t"), 1)
            pe.wait_ge(sem("sd_wide"), 1)
            for c in range(KC):
                last = nc.tensor.transpose(bank[1][:, c * P:(c + 1) * P], xq_f[0][:, c * P:(c + 1) * P], ident[:, :])
            last.then_inc(sem("sd_t"), 1)

        def weights_act(act):
            bb = bank[0][:, :].bitcast(bf16)
            for n in range(3):
                for half in range(2):
                    act.wait_ge(sem("w_half_t"), 2 * n + half + 1)
                    src = bb[:, 0:IC * P]
                    if n < 2:
                        last = nc.scalar.copy((wgi, wui)[n][:, half, :], src)
                    else:
                        last = nc.scalar.copy(wdi[:, :, half * P:(half + 1) * P], src.rearrange("p (c i) -> p c i", c=IC))
                    last.then_inc(sem("w_half_out"), 1)
                act.drain().then_inc(sem("w_t_out"), 1)

        def ffn_chunks(eng, body, name_first, extra):
            slots(eng, body, NC_, 4, 4 + max(0, (NC_ - 4) // 4 * 4), 0, NC_ + extra, 4)

        def ffn_pe(pe, pas):
            def xq_t(c):
                if c is None or pas:
                    return
                b, r = c
                wait(pe, "xq_done", b + 1)
                wait(pe, "xqt_out", b)
                bb = bank[6][:, :].bitcast(bf16)
                for k in range(KC):
                    for t in range(TPC):
                        last = nc.tensor.transpose(bb[:, k * CT + t * P:k * CT + (t + 1) * P],
                                                   xq_b[r % 2][:, t, k * P:(k + 1) * P], identb[:, :])
                last.then_inc(sem("xq_t"), 1)

            def gate_up(c):
                if c is None:
                    return
                b, r = c
                if not pas:
                    wait(pe, "xqt_out", b + 1)
                for i in range(IC):
                    g, u = bank[2 * (i % GUB)], bank[2 * (i % GUB) + 1]
                    wait(pe, f"f_h_done{pas}", IC * b + i - GUB + 1)
                    for k in range(KC):
                        nc.tensor.matmul(g[:, :], wgi[:, k, i * P:(i + 1) * P], xqt[:, k, bass.ds(b * CT, CT)],
                                         start=(k == 0), stop=(k == KC - 1))
                    for k in range(KC):
                        last = nc.tensor.matmul(u[:, :], wui[:, k, i * P:(i + 1) * P], xqt[:, k, bass.ds(b * CT, CT)],
                                                start=(k == 0), stop=(k == KC - 1))
                    last.then_inc(sem(f"f_gu_done{pas}"), 1)

            def down(c):
                if c is None or not pas:
                    return
                b, r = c
                wait(pe, "f_q_done", IC * b + IC)
                for t in range(TPC):
                    wait(pe, "f_y_read", TPC * b + t - 1)
                    for i in range(IC):
                        last = nc.tensor.matmul(bank[6 + t % 2][:, 0:D], f_q[r % 2][:, i, t * P:(t + 1) * P], wdi[:, i, :],
                                                start=(i == 0), stop=(i == IC - 1))
                    last.then_inc(sem("f_down_done"), 1)

            def body(stage):
                xq_t(stage(0))
                gate_up(stage(0) if pas else stage(1))
                down(stage(1))
            ffn_chunks(pe, body, 0, 1)

        def ffn_act(act, pas):
            def copy_t(c):
                if c is None or pas:
                    return
                b, r = c
                wait(act, "xq_t", b + 1)
                nc.scalar.copy(xqt[:, :, bass.ds(b * CT, CT)], bank[6][:, :].bitcast(bf16).rearrange("p (k t) -> p k t", k=KC)
                               ).then_inc(sem("xqt_out"), 1)

            def silu(c):
                if c is None:
                    return
                b, r = c
                for i in range(IC + 1):
                    if i < IC:
                        wait(act, f"f_gu_done{pas}", IC * b + i + 1)
                        wait(act, f"f_h_done{pas}", IC * b + i - 2)
                        nc.scalar.activation(f_sg[i % 3][:, :], bank[2 * (i % GUB)][:, :], ACT.Silu,
                                             scale=s_gux[:, 0, i:i + 1]).then_inc(sem(f"f_sg_done{pas}"), 1)
                    if pas and i >= 1:
                        j = i - 1
                        wait(act, "f_clip_done", IC * b + j + 1)
                        if j == 0:
                            wait(act, "f_down_done", TPC * (b - 1))
                        nc.scalar.activation(f_q[r % 2][:, j, :], f_h[j % 3][:, :], ACT.Copy, bias=-RND).then_inc(sem("f_q_done"), 1)

            def body(stage):
                copy_t(stage(0))
                silu(stage(0) if pas else stage(1))
            ffn_chunks(act, body, 0, 1)

        def ffn_pool(pool):
            def clip(c):
                if c is None:
                    return
                b, r = c
                for i in range(IC):
                    wait(pool, "f_scaled", IC * b + i + 1)
                    hold(pool)
                    nc.gpsimd.tensor_scalar(f_h[i % 3][:, :], f_h[i % 3][:, :], -QMAX - 1.0, RND, ALU.max, ALU.add
                                            ).then_inc(sem("f_clip_done"), 1)

            ffn_chunks(pool, lambda stage: clip(stage(0)), 0, 1)

        def ffn_dve(dve, pas):
            V = nc.vector

            def quantise(c):
                if c is None or pas:
                    return
                b, r = c
                p = r % 2
                st = Steps(dve, "xq_step", 2, b)
                src = big[:, bass.ds(b * (TPC * D), TPC * D)]
                st.then(V.tensor_scalar(xq_f[p][:, :], src, scl[:, 1:2], RND, ALU.mult, ALU.add))
                st.then(V.tensor_scalar(xq_f[p][:, :], xq_f[p][:, :], RND + QMAX, RND - QMAX - 1.0, ALU.min, ALU.max))
                wait(dve, "xq_t", b - 1)
                V.tensor_scalar(xq_b[p][:, :, :].rearrange("p t d -> p (t d)"), xq_f[p][:, :], -RND, None, ALU.add).then_inc(sem("xq_done"), 1)
                st.end()

            def hidden(c):
                if c is None:
                    return
                b, r = c
                st = Steps(dve, f"f_step{pas}", IC + (0 if pas else 1), b)
                for i in range(IC):
                    wait(dve, f"f_sg_done{pas}", IC * b + i + 1)
                    if pas:
                        wait(dve, "f_q_done", IC * b + i - 2)
                    h = V.scalar_tensor_tensor(f_h[i % 3][:, :], bank[2 * (i % GUB) + 1][:, :], s_gux[:, 1, i:i + 1],
                                               f_sg[i % 3][:, :], ALU.mult, ALU.mult)
                    if pas:
                        st.then(h)
                        dve.sem_inc(sem("f_h_done1"), 1)
                        V.tensor_scalar(f_h[i % 3][:, :], f_h[i % 3][:, :], scl[:, 3:4], QMAX, ALU.mult, ALU.min).then_inc(sem("f_scaled"), 1)
                    else:
                        st.then(h)
                        V.tensor_reduce(hmax[:, 1, i:i + 1], f_h[i % 3][:, :], AX, ALU.max,
                                        apply_absolute_value=True).then_inc(sem("f_h_done0"), 1)
                if not pas:
                    dve.wait_ge(sem("f_h_done0"), IC * b + IC)
                    st.then(V.tensor_tensor(hmax[:, 0, :], hmax[:, 0, :], hmax[:, 1, :], ALU.max))
                st.end()

            def outputs(c):
                if c is None or not pas:
                    return
                b, r = c
                st = Steps(dve, "f_out_step", TPC, b)
                for t in range(TPC):
                    wait(dve, "f_down_done", TPC * b + t + 1)
                    st.then(V.tensor_tensor(yo[t % 2][:, :], bank[6 + t % 2][:, 0:D], sd_row[:, :], ALU.mult))
                    dve.sem_inc(sem("f_y_read"), 1)
                    wait(dve, f"f_stored{t}", 16 * b)
                    V.tensor_tensor(yo2[t][:, :], yo[t % 2][:, :], res[:, bass.ds(b * TPC + t, 1), :].rearrange("p o d -> p (o d)"),
                                    ALU.add).then_inc(sem("f_y_done"), 1)
                st.end()

            def body(stage):
                quantise(stage(0))
                hidden(stage(0) if pas else stage(1))
                outputs(stage(1))
            ffn_chunks(dve, body, 0, 1)

        def ffn_sp(sp):
            out_v = out.rearrange("b s d -> s b d")

            def store(c):
                if c is None:
                    return
                b, r = c
                for t in range(TPC):
                    wait(sp, "f_y_done", TPC * b + t + 1)
                    hold(sp)
                    sp.dma_start(out_v[:, bass.ds(b * TPC + t, 1), :].rearrange("s o d -> s (o d)"), yo2[t][:, :]
                                 ).then_inc(sem(f"f_stored{t}"), 16)

            ffn_chunks(sp, lambda stage: store(stage(1)), 0, 1)
            for t in range(TPC):
                sp.wait_ge(sem(f"f_stored{t}"), 16 * NC_)

        def attention_weights(eng, L, name):
            n = (("L0_xattn_wq_w", "L0_xattn_wk_w", "L0_xattn_wv_w", "L0_xattn_wo_w"),
                 ("L1_xattn_wq", "L1_xattn_wk", "L1_xattn_wv", "L1_xattn_wo"))[L]
            v = (("L0_xattn_wq_b", "L0_xattn_wk_b", "L0_xattn_wv_b", "L0_xattn_wo_b"),
                 ("L1_xattn_bq", "L1_xattn_bk", "L1_xattn_bv", "L1_xattn_bo"))[L]
            for dst, src in zip((w_q, w_k, w_v, w_o), n):
                eng.dma_start(dst[:, :, :], a[src].rearrange("(k p) n -> p k n", p=P)).then_inc(sem(name), 16)
            for c, src in enumerate(v[:2]):
                eng.dma_start(qk_bias[:, c * KC:(c + 1) * KC], a[src].rearrange("(k p) -> p k", p=P),
                              allow_slow_non_contiguous=True).then_inc(sem(name), 16)
            for dst, src in zip((v_bias, o_bias), v[2:]):
                eng.dma_start(dst[:, :], a[src].unsqueeze(0).broadcast_to([P, D])).then_inc(sem(name), 16)

        block = ctx.enter_context(nc.Block())

        @block.sync
        def _(sp):
            attention_weights(sp, 0, "w_in")
            for n, g in enumerate(("g_xattn", "g_ffn")):
                sp.dma_start(gates[:, 2 * n:2 * n + 2], a[g].unsqueeze(0).broadcast_to([P, 2])).then_inc(sem("w_in"), 16)
            sp.dma_start(ebias[:, :], a["L0_ffn_e_bias"].unsqueeze(0).broadcast_to([P, E])).then_inc(sem("w_in"), 16)
            for dst, src in ((w_gate, "L0_ffn_gate_weight"), (w_sg, "L0_ffn_shared_gate"), (w_su, "L0_ffn_shared_up"),
                             (w_sd, "L0_ffn_shared_down")):
                sp.dma_start(dst[:, :, :], a[src].rearrange("(k p) n -> p k n", p=P)).then_inc(sem("w_in"), 16)
            sp.dma_start(mask_i[:, :], a["mask_1x1xSxS2_ik0"].rearrange("a b q k -> (a b q) k")).then_inc(sem("w_in"), 16)
            phase_end(sp, 1)
            attention_sp(sp, 0)
            for p in range(2):
                sp.wait_ge(sem(f"xa_stored{p}"), 8 * NB)
            phase_end(sp, 2)
            attention_weights(sp, 1, "w1_in")
            experts_sp(sp)
            phase_end(sp, 3)
            attention_sp(sp, 1)
            phase_end(sp, 4)
            for n, src in enumerate(("L1_ffn_w_gate", "L1_ffn_w_up")):
                sp.dma_start(wraw[n][:, 0:IFULL, :], a[src][0:IFULL * P, :].rearrange("(c p) d -> p c d", p=P)).then_inc(sem("ffn_w_in"), 16)
                if IREST:
                    sp.dma_start(wraw[n][0:IREST, IFULL, :], a[src][IFULL * P:I, :]).then_inc(sem("ffn_w_in"), 16)
            sp.dma_start(wdraw[:, :, :], a["L1_ffn_w_down"].rearrange("(k p) i -> p k i", p=P)).then_inc(sem("ffn_w_in"), 16)
            sp.dma_start(clips[:, 0:1], a["L1_ffn_clip_x"].unsqueeze(0).broadcast_to([P, 1])).then_inc(sem("clip_in"), 16)
            sp.dma_start(clips[:, 1:2], a["L1_ffn_clip_down"].unsqueeze(0).broadcast_to([P, 1])).then_inc(sem("clip_in"), 16)
            phase_end(sp, 5)
            phase_end(sp, 6)
            ffn_sp(sp)

        @block.gpsimd
        def _(pool):
            G = nc.gpsimd
            G.iota(slot_base_i[:, :], [[CAP, E]], base=1, channel_multiplier=0)
            G.iota(tok_i[:, :], [[P, 2]], base=DUMP, channel_multiplier=1).then_inc(sem("iota_done"), 1)
            G.memset(ident[:, :], 0.0)
            G.memset(onesb[:, :], 1.0).then_inc(sem("pool_set"), 1)
            pool.wait_ge(sem("pool_set"), 1)
            G.affine_select(out=ident[:, :], in_=ident[:, :], compare_op=ALU.not_equal, fill=1.0, base=0,
                            pattern=[[-1, P]], channel_multiplier=1).then_inc(sem("pool_made"), 1)
            G.affine_select(out=strict_tri[:, :], in_=onesb[:, :], compare_op=ALU.is_gt, fill=0.0, base=0,
                            pattern=[[1, P]], channel_multiplier=-1).then_inc(sem("pool_made"), 1)
            phase_end(pool, 1)
            xe_v = xe.rearrange("(n e h p) c -> n p e h c", n=8, p=P, h=HALVES)
            for n in range(8):
                for h in range(HALVES):
                    G.dma_start(xe_v[n, :, :, h, :], zt[:, h, :].unsqueeze(1).broadcast_to([P, E // 8, ROW])).then_inc(sem("xe_zero"), 16)
            G.dma_start(acc[1].rearrange("(n p) d -> p n d", p=P), zt[:, 0, 0:D].unsqueeze(1).broadcast_to([P, NB + HALVES, D])
                        ).then_inc(sem("acc_zero"), 16)
            G.dma_start(acc[0][T:T + HALVES * P, :].rearrange("(n p) d -> p n d", p=P), zt[:, :, 0:D]).then_inc(sem("acc_zero"), 16)
            pool.wait_ge(sem("xe_zero"), 16 * 8 * HALVES)

            def scatter(k):
                if k is None:
                    return
                b, r = k
                pool.wait_ge(sem("idx_done_0"), b + 1)
                hold(pool)
                for n in range(TOPK):
                    G.indirect_dma_start(out=xe[:, :], out_offset=bass.IndirectOffsetOnAxis(ap=idx[r][:, n:n + 1], axis=0),
                                         in_=pay[r][:, :], in_offset=None, bounds_check=E * CAP - 1,
                                         oob_is_err=False).then_inc(sem(f"scattered{r}"), 16)

            attention_slots(pool, lambda stage: scatter(stage(4)))
            for r in range(4):
                pool.wait_ge(sem(f"scattered{r}"), 32 * NB)
            pool.wait_ge(sem("acc_zero"), 32)
            phase_end(pool, 2)
            experts_pool(pool)
            phase_end(pool, 3)
            phase_end(pool, 4)
            ReduceOp = bass.bass_isa.ReduceOp
            pool.wait_ge(sem("amax_done"), 1)
            G.partition_all_reduce(gmax[:, 0:1], amax[:, 0:1], P, ReduceOp.max).then_inc(sem("gmax_done"), 1)
            phase_end(pool, 5)
            pool.wait_ge(sem("hmax_done"), 1)
            G.partition_all_reduce(gmax[:, 1:2], amax[:, 1:2], P, ReduceOp.max).then_inc(sem("gmax_done"), 1)
            phase_end(pool, 6)
            ffn_pool(pool)

        @block.scalar
        def _(act):
            act.wait_ge(sem("w_in"), 16 * 16)
            nc.scalar.activation(tg[:, :], gates[:, :], ACT.Tanh).then_inc(sem("tg_done"), 1)
            phase_end(act, 1)
            attention_act(act, 0)
            phase_end(act, 2)
            experts_act(act)
            phase_end(act, 3)
            attention_act(act, 1)
            phase_end(act, 4)
            act.wait_ge(sem("clip_in"), 32)
            nc.scalar.activation(sig[:, :], clips[:, :], ACT.Exp, scale=-1.0).then_inc(sem("sig_done"), 1)
            weights_act(act)
            act.wait_ge(sem("sx_done"), 1)
            ffn_act(act, 0)
            phase_end(act, 5)
            phase_end(act, 6)
            ffn_act(act, 1)

        @block.tensor
        def _(pe):
            phase_end(pe, 1)
            attention_pe(pe, 0)
            phase_end(pe, 2)
            experts_pe(pe)
            phase_end(pe, 3)
            attention_pe(pe, 1)
            phase_end(pe, 4)
            weights_pe(pe)
            ffn_pe(pe, 0)
            phase_end(pe, 5)
            phase_end(pe, 6)
            ffn_pe(pe, 1)

        @block.vector
        def _(dve):
            V = nc.vector
            for k in range(2):
                V.memset(kbd[k][:, :, :], 0.0)
                V.memset(vx[k][:, :, DH:32], 0.0)
            V.memset(eps_col[:, :], EPS)
            V.memset(zt[:, :, :], 0.0)
            V.memset(count[:, :], 0.0)
            V.memset(gs[:, EG:EG + 4], LOW)
            V.memset(tog[:, GSEL:8], LOW)
            V.memset(mv[:, :, :], 1.0)
            for r in range(4):
                V.memset(pay[r][:, TOKC:ROW], 0.0)
            st = Steps(dve, "set_step", 5, 0)
            st.then(V.memset(amax[:, :], 0.0))
            for k in range(2):
                V.memset(vx[k][:, :, DH:DH + 1], 1.0)
            dve.wait_ge(sem("pool_made"), 2)
            V.tensor_copy(identb[:, :], ident[:, :])
            dve.wait_ge(sem("iota_done"), 1)
            V.tensor_copy(slot_base[:, :], slot_base_i[:, :])
            st.then(V.tensor_copy(zt[:, :, TOKC], tok_i[:, :]))
            for r in range(4):
                V.tensor_scalar(pay[r][:, TOKC:TOKC + 1], zt[:, 0, TOKC:TOKC + 1], float((r - 4) * P - DUMP), None, ALU.add)
            dve.wait_ge(sem("w_in"), 16 * 16)
            st.then(V.tensor_scalar(mask_bias[:, :], mask_i[:, :], 0, NEG, ALU.is_equal, ALU.mult))
            dve.wait_ge(sem("tg_done"), 1)
            V.tensor_scalar(tg_half[:, :], tg[:, 2:3], 0.5, None, ALU.mult)
            V.tensor_scalar(tg_route[:, :], tg[:, 2:3], ROUTE_SCALE, None, ALU.mult)
            st.then(V.tensor_scalar(o_bias[:, :], o_bias[:, :], tg[:, 0:1], None, ALU.mult))
            st.then(V.memset(hmax[:, :, :], 0.0))
            st.end()
            phase_end(dve, 1)
            attention_dve(dve, 0)
            phase_end(dve, 2)
            dve.wait_ge(sem("w1_in"), 16 * 8)
            V.tensor_scalar(o_bias[:, :], o_bias[:, :], tg[:, 1:2], None, ALU.mult)
            experts_dve(dve)
            phase_end(dve, 3)
            attention_dve(dve, 1)
            dve.wait_ge(sem("xn2_done_1"), NB)
            V.tensor_reduce(amax[:, 0:1], big[:, 0:NB * D], AX, ALU.max, apply_absolute_value=True).then_inc(sem("amax_done"), 1)
            phase_end(dve, 4)
            if IREST:
                for n in range(2):
                    last = V.memset(wraw[n][IREST:P, IFULL, :], 0.0)
                last.then_inc(sem("pad_set"), 1)
                dve.wait_ge(sem("pad_set"), 1)
            weights_dve(dve)
            dve.wait_ge(sem("sx_done"), 1)
            V.tensor_copy(xq_f[0][:, 0:D].rearrange("p (c o) -> p c o", c=KC),
                          s_d[:, :].unsqueeze(2).broadcast_to([P, KC, P])).then_inc(sem("sd_wide"), 1)
            dve.wait_ge(sem("sd_t"), 1)
            V.tensor_copy(sd_row[:, :], bank[1][:, 0:D])
            ffn_dve(dve, 0)
            dve.wait_ge(sem("f_step0"), (IC + 1) * NC_)
            V.tensor_reduce(amax[:, 1:2], hmax[:, 0, :], AX, ALU.max).then_inc(sem("hmax_done"), 1)
            phase_end(dve, 5)
            st = Steps(dve, "sh_step", 4, 0)
            dve.wait_ge(sem("gmax_done"), 2)
            st.then(V.tensor_scalar(scl[:, 2:3], gmax[:, 1:2], sig[:, 1:2], 1.0 / QMAX, ALU.mult, ALU.mult))
            st.then(V.reciprocal(scl[:, 3:4], scl[:, 2:3]))
            st.then(V.tensor_scalar(scl[:, 4:5], scl[:, 2:3], tg[:, 3:4], None, ALU.mult))
            st.then(V.tensor_scalar(sd_row[:, :], sd_row[:, :], scl[:, 4:5], None, ALU.mult))
            st.end()
            phase_end(dve, 6)
            ffn_dve(dve, 1)


_TRANSPOSED = ("L0_xattn_wq_w", "L0_xattn_wk_w", "L0_xattn_wv_w", "L0_xattn_wo_w", "L0_ffn_gate_weight", "L0_ffn_w1",
               "L0_ffn_w2", "L0_ffn_w3", "L0_ffn_shared_gate", "L0_ffn_shared_up", "L0_ffn_shared_down",
               "L1_xattn_wq", "L1_xattn_wk", "L1_xattn_wv", "L1_xattn_wo")


def kernel(**inputs):
    import numpy as np
    import concourse.bacc as bacc
    from concourse.bass_utils import run_bass_kernel_spmd

    nc = bacc.Bacc("TRN2", target_bir_lowering=False, num_devices=1)
    arrays, aps = {}, {}
    for name, value in inputs.items():
        v = np.asarray(value)
        if name in _TRANSPOSED:
            v = np.swapaxes(v, -1, -2)
        v = np.ascontiguousarray(v)
        arrays[f"in_{name}"] = v
        aps[name] = nc.dram_tensor(f"in_{name}", v.shape, mybir.dt.from_np(v.dtype), kind="ExternalInput").ap()
    out = nc.dram_tensor("out_0", arrays["in_x"].shape, mybir.dt.float32, kind="ExternalOutput").ap()
    flamingo_gated_two_layers(nc, aps, out)
    result = run_bass_kernel_spmd(nc, [arrays], core_ids=[0])
    return result.results[0]["out_0"]
```

```python
import concourse.bass as bass
from concourse import mybir
from contextlib import ExitStack


def flamingo_gated_two_layers(nc: bass.Bass, a, out: bass.AP):
    f32, bf16, i32 = mybir.dt.float32, mybir.dt.bfloat16, mybir.dt.int32
    ALU = mybir.AluOpType
    ACT = mybir.ActivationFunctionType
    AX = mybir.AxisListType.X

    NB, S, D = a["x"].shape
    P = 128
    H = 16
    DH = D // H
    KC = D // P
    HB = P // DH
    GH = 4
    NG = H // GH
    SM_SCALE = float(DH) ** -0.5
    EPS = 1e-5
    T = NB * S
    E, F = a["L0_ffn_w1"].shape[0], a["L0_ffn_w1"].shape[2]
    CAP, TOPK, EG, GSEL, ROUTE_SCALE = 256, 8, 8, 4, 2.5
    EPG = E // EG
    HALVES = CAP // P
    FS = a["L0_ffn_shared_gate"].shape[1]
    ROW = D + E + 4
    TOKC = D + E
    DUMP = T
    I = a["L1_ffn_w_gate"].shape[0]
    IC = (I + P - 1) // P
    IFULL, IREST = I // P, I % P
    CT = 512
    NC_ = T // CT
    TPC = CT // P
    QMAX = 127.0
    RND = 12582912.0
    NEG = -(2.0 ** 60)
    LOW = -1.0e30
    NORM_STEPS = 13

    SLOT0, LAGS, UNROLL = 8, 5, 4
    LOOP_END = SLOT0 + max(0, (NB - 2 - SLOT0) // UNROLL * UNROLL)

    xe = nc.dram_tensor("expert_rows", [E * CAP, ROW], f32).ap()
    acc = [nc.dram_tensor(f"accumulator_{n}", [T + HALVES * P, D], f32).ap() for n in range(2)]

    ctx = ExitStack()
    with ctx:
        region = [ctx]

        def sb(name, shape, dt=f32):
            return region[0].enter_context(nc.sbuf_tensor(name, shape, dt))

        def ring(name, n, shape, dt=f32):
            return [sb(f"{name}{k}", shape, dt) for k in range(n)]

        sems = {}

        def sem(name):
            if name not in sems:
                sems[name] = ctx.enter_context(nc.semaphore(name))
            return sems[name]

        bank = [ctx.enter_context(nc.psum_tensor(f"bank{k}", [P, 512], f32)) for k in range(8)]

        ident = sb("ident", [P, P])
        identb = sb("identb", [P, P], bf16)
        strict_tri = sb("strict_tri", [P, P], bf16)
        onesb = sb("onesb", [P, P], bf16)
        gates = sb("gates", [P, 4])
        tg = sb("tg", [P, 4])
        tg_half = sb("tg_half", [P, 1])
        tg_route = sb("tg_route", [P, 1])
        mask_bias = sb("mask_bias", [P, S], bf16)

        clips = sb("clips", [P, 2])
        sig = sb("sig", [P, 2])
        amax = sb("amax", [P, 2])
        gmax = sb("gmax", [P, 2])
        scl = sb("scl", [P, 5])
        hmax = sb("hmax", [P, NC_ * IC])
        tmax = sb("tmax", [P, NB])
        res = sb("res", [P, NB, D])

        moe_region = ExitStack()
        region[0] = moe_region
        ebias = sb("ebias", [P, E])
        slot_base = sb("slot_base", [P, E])
        slot_base_i = sb("slot_base_i", [P, E], i32)
        tok_i = sb("tok_i", [P, 2], i32)
        mask_i = sb("mask_i", [P, S], i32)
        zt = sb("zt", [P, HALVES, ROW])
        w_gate = sb("w_gate", [P, KC, E])
        w_sg, w_su = sb("w_sg", [P, KC, FS]), sb("w_su", [P, KC, FS])
        w_sd = sb("w_sd", [P, FS // P, D])
        pay = ring("pay", 4, [P, ROW])
        x2t = ring("x2t", 2, [P, KC, P])
        en = ring("en", 2, [P, E])
        th = ring("th", 2, [P, FS])
        hs = sb("hs", [P, FS])
        ht = ring("ht", 2, [P, FS // P, P])
        sfc, score, tmp, rep = (sb(n, [P, E]) for n in ("sfc", "score", "tmp", "rep"))
        sel = ring("sel", 2, [P, E], bf16)
        self_ = sb("self_", [P, E])
        wun = sb("wun", [P, E])
        wsum = sb("wsum", [P, 1])
        m8 = sb("m8", [P, EG, 8])
        gs = sb("gs", [P, EG + 4])
        top = sb("top", [P, 8])
        tog = sb("tog", [P, 8])
        grep = sb("grep", [P, EG + 4])
        gmask = sb("gmask", [P, EG, 1])
        count = sb("count", [P, E])
        pos, key, valid = (sb(n, [P, E]) for n in ("pos", "key", "valid"))
        keys8 = sb("keys8", [P, 8])
        far = sb("far", [P, 8])
        idx = ring("idx", 4, [P, TOPK], i32)
        xa = ring("xa", 2, [P, D])

        xr = ring("xr", 4, [P, HALVES, ROW])
        xrt = ring("xrt", 2, [P, KC, CAP])
        sg = ring("sg", 2, [P, CAP])
        he = ring("he", 2, [P, CAP])
        ye = ring("ye", 4, [P, HALVES, D])
        wcol = ring("wcol", 4, [P, HALVES])
        tid = ring("tid", 4, [P, HALVES], i32)

        moe_region.close()
        region[0] = ctx
        MOE_BYTES = 60 * 1024
        big = sb("big", [P, max(NB * D, MOE_BYTES // 4)])
        xn3 = big[:, 0:NB * D].rearrange("p (b d) -> p b d", b=NB)
        attention_region = ExitStack()
        region[0] = attention_region
        w_q, w_k, w_v, w_o = (sb(f"w_{n}", [P, KC, D]) for n in "qkvo")
        bias = sb("bias", [P, 4 * D])
        bias_part = sb("bias_part", [P, 4 * D], bf16)
        bias3 = sb("bias3", [P, 4 * D], bf16)

        cx = ring("cx", 4, [P, KC, P])
        ax = ring("ax", 2, [P, 2, D])
        xn = ring("xn", 2, [P, D])
        xt = ring("xt", 2, [P, KC, P])
        qk = ring("qk", 2, [P, 2 * KC, P])
        kbd = ring("kbd", 2, [P, KC, HB * P])
        vx = ring("vx", 2, [P, H, 32])
        sc = ring("sc", 4, [P, GH, P])
        pt = ring("pt", 2, [P, GH, P])
        mx = sb("mx", [P, H])
        ov = ring("ov", 2, [P, NG, P])
        rden = sb("rden", [P, H, 1])
        on = ring("on", 2, [P, D])
        at = ring("at", 2, [P, KC, P])
        st1, st2 = sb("st1", [P, 6]), sb("st2", [P, 6])
        mv = sb("mv", [P, 2, 2])
        var, root, newton = (sb(n, [P, 2]) for n in ("var", "root", "newton"))
        rstd = sb("rstd", [P, 2])
        nmr = sb("nmr", [P, 2])
        assert 2 * KC <= GH and F <= P
        wa = [sc[k][:, 0:KC, 0:F] for k in range(4)]
        wb = [sc[k][:, KC:2 * KC, 0:F] for k in range(4)]
        wc = [k[:, :] for k in xn + on]
        attention_region.close()
        region[0] = ctx
        IP = IC * P
        wgi = sb("wgi", [P, KC, IP], bf16)
        wui = sb("wui", [P, KC, IP], bf16)
        wdi = sb("wdi", [P, IC, D], bf16)
        wq_b = sb("wq_b", [P, KC * IP], bf16)
        s_gu = sb("s_gu", [P, 2, IC])
        s_gux = sb("s_gux", [P, 2, IC])
        s_guq = sb("s_guq", [P, IC])
        s_d = sb("s_d", [P, KC])
        inv = sb("inv", [P, 4 * IC])
        sd_row = sb("sd_row", [P, D])
        xq_f = ring("xq_f", 2, [P, TPC * D])
        xq_b = ring("xq_b", 2, [P, TPC, D], bf16)
        f_sg = ring("f_sg", 3, [P, CT])
        f_h = ring("f_h", IC, [P, CT])
        f_q = [big[:, n * IC * CT // 2:(n + 1) * IC * CT // 2].bitcast(bf16).rearrange("p (c t) -> p c t", c=IC) for n in range(2)]
        yo = [xq_b[t // 2][:, :, :].rearrange("p t d -> p (t d)").bitcast(f32)[:, t % 2 * D:(t % 2 + 1) * D] for t in range(TPC)]
        assert TPC * D // 2 >= 2 * D and TPC == 4
        W_BYTES = 4 * (2 * IC * D + KC * I)
        xqt_all = sb("xqt", [P, max(KC * T, W_BYTES // 2)], bf16)
        xqt = xqt_all[:, 0:KC * T].rearrange("p (k t) -> p k t", k=KC)
        raw = xqt_all[:, 0:W_BYTES // 2].bitcast(f32)
        wraw = [raw[:, n * IC * D:(n + 1) * IC * D].rearrange("p (c d) -> p c d", c=IC) for n in range(2)]
        wdraw = raw[:, 2 * IC * D:2 * IC * D + KC * I].rearrange("p (k i) -> p k i", k=KC)

        def phase_end(eng, n):
            eng.drain().then_inc(sem("phase_done"), 1)
            eng.wait_ge(sem("phase_done"), 5 * n)

        def wait(eng, name, value):
            if not (isinstance(value, int) and value <= 0):
                eng.wait_ge(sem(name), value)

        def row(b):
            return res[:, bass.ds(b, 1), :].rearrange("p o d -> p (o d)")

        def hold(eng):
            eng.sem_inc(sem("held"), 1)

        def ahead(b, n):
            return min(b + n, NB) if isinstance(b, int) else b + n

        class Steps:

            def __init__(self, eng, name, n, b):
                self.eng, self.name, self.n, self.b, self.k = eng, name, n, b, 0

            def mark(self, ins):
                self.k += 1
                assert self.k <= self.n, self.name
                ins.then_inc(sem(self.name), 1)

            def need(self):
                self.eng.wait_ge(sem(self.name), self.b * self.n + self.k)

            def then(self, ins):
                self.mark(ins)
                self.need()

            def end(self):
                assert self.k == self.n, (self.name, self.k)

        def slots(eng, body, nb, slot0, loop_end, first, last, unroll):
            def at_slot(s):
                def stage(lag):
                    b = s - lag
                    return (b, b % 4) if 0 <= b < nb else None
                body(stage)
            for s in range(first, min(slot0, last)):
                at_slot(s)
            if loop_end > slot0:
                assert (loop_end - slot0) % unroll == 0
                with eng.Fori(slot0, loop_end - unroll + 1, unroll) as i:
                    for u in range(unroll):
                        body(lambda lag, u=u: (i + (u - lag), (slot0 + u - lag) % 4))
            for s in range(max(loop_end, slot0), last):
                at_slot(s)

        def attention_slots(eng, body):
            slots(eng, body, NB, SLOT0, LOOP_END, -1, NB + LAGS, UNROLL)


        def attention_pe(pe, L):
            def sm(name):
                return f"{name}_{L}"

            def scores(m, g):
                if m is None:
                    return
                b, r = m
                p, j = r % 2, g // (NG // KC)
                if g == 0:
                    pe.wait_ge(sem(sm(f"kbd_in{p}")), 64 * (b - p) + 128)
                bk = bank[g % 2]
                wait(pe, sm("exp_done"), 4 * b + g - 1)
                if L == 1:
                    nc.tensor.matmul(bk[:, :], identb[:, :], mask_bias[:, :].unsqueeze(1).broadcast_to([P, GH, S]),
                                     start=True, stop=False)
                c0 = (g % (NG // KC)) * GH * P
                nc.tensor.matmul(bk[:, :], qk[p][:, j, :], kbd[p][:, j, c0:c0 + GH * P],
                                 start=(L == 0), stop=True).then_inc(sem(sm("s_done")), 1)

            def probs_t(m, g):
                if m is None:
                    return
                b, _ = m
                pe.wait_ge(sem(sm("exp_done")), 4 * b + g + 1)
                wait(pe, sm("pt_out"), 4 * b + g - 1)
                for h in range(GH):
                    last = nc.tensor.transpose(bank[2 + g % 2][:, h * P:(h + 1) * P], sc[g][:, h, :], ident[:, :])
                last.then_inc(sem(sm("pt_done")), 1)

            def values(m, g):
                if m is None:
                    return
                b, r = m
                p = r % 2
                pe.wait_ge(sem(sm("pt_out")), 4 * b + g + 1)
                if g == 0:
                    pe.wait_ge(sem(sm("v_out")), b + 1)
                    wait(pe, sm("ov_out"), b)
                for h in range(GH):
                    last = nc.tensor.matmul(bank[7][32 * h:32 * h + 32, g * P:(g + 1) * P], vx[p][:, GH * g + h, :],
                                            pt[g % 2][:, h, :], start=True, stop=True)
                last.then_inc(sem(sm("pv_done")), 1)

            def transposes(f):
                if f is None:
                    return
                b, r = f
                p = r % 2
                pe.wait_ge(sem(sm("xn1_done")), b + 1)
                wait(pe, sm("at_out"), b - 2)
                if L == 0:
                    wait(pe, sm("en_out"), b - 3)
                for c in range(KC):
                    last = nc.tensor.transpose(bank[4][:, c * P:(c + 1) * P], xn[p][:, c * P:(c + 1) * P], ident[:, :])
                last.then_inc(sem(sm("t_done")), 1)

            def project_qk(f):
                if f is None:
                    return
                b, r = f
                p = r % 2
                pe.wait_ge(sem(sm("xt_out")), b + 1)
                pe.wait_ge(sem(sm(f"tile_in{r}")), (2 - L) * (4 * (b - r) + 16))
                if L == 0:
                    wait(pe, sm("silu_done"), b - 3)
                else:
                    wait(pe, sm("qk_out"), b)
                for n, w in enumerate((w_q, w_k)):
                    for j in range(KC):
                        o_ = bank[5][:, (n * KC + j) * P:(n * KC + j + 1) * P]
                        nc.tensor.matmul(o_, bias3[:, n * D + j * P:n * D + (j + 1) * P], onesb[:, :], start=True, stop=False)
                        for c in range(KC):
                            last = nc.tensor.matmul(o_, w[:, c, j * P:(j + 1) * P], (cx[r] if n else xt[p])[:, c, :],
                                                    start=False, stop=(c == KC - 1))
                last.then_inc(sem(sm("qk_done")), 1)

            def project_v(f):
                if f is None:
                    return
                b, r = f
                p = r % 2
                wait(pe, sm("x3_done"), b - 2)
                if L == 0:
                    wait(pe, sm("pos_done"), b - 4)
                nc.tensor.matmul(bank[6][:, 0:D], onesb[:, :], bias3[:, 2 * D:3 * D], start=True, stop=False)
                for c in range(KC):
                    last = nc.tensor.matmul(bank[6][:, 0:D], cx[r][:, c, :], w_v[:, c, :],
                                            start=False, stop=(c == KC - 1))
                last.then_inc(sem(sm("v_done")), 1)

            def output(k):
                if k is None:
                    return
                b, r = k
                pe.wait_ge(sem(sm("at_out")), b + 1)
                pe.wait_ge(sem(sm("v_out")), ahead(b, 3))
                if L == 0:
                    wait(pe, sm("pos_done"), b - 2)
                nc.tensor.matmul(bank[6][:, 0:D], onesb[:, :], bias3[:, 3 * D:4 * D], start=True, stop=False)
                for c in range(KC):
                    last = nc.tensor.matmul(bank[6][:, 0:D], at[r % 2][:, c, :], w_o[:, c, :],
                                            start=False, stop=(c == KC - 1))
                last.then_inc(sem(sm("o_done")), 1)

            def heads_to_tokens(k):
                if k is None:
                    return
                b, r = k
                pe.wait_ge(sem(sm("ov_out")), b + 1)
                pe.wait_ge(sem(sm("xt_out")), ahead(b, 3))
                if L == 0:
                    wait(pe, sm("xa_done"), b - 1)
                for g in range(NG):
                    last = nc.tensor.transpose(bank[4][:, g * P:(g + 1) * P], ov[r % 2][:, g, :], ident[:, :])
                last.then_inc(sem(sm("ot_done")), 1)

            def tokens_to_heads(k):
                if k is None:
                    return
                b, r = k
                pe.wait_ge(sem(sm("on_done")), b + 1)
                for c in range(KC):
                    last = nc.tensor.transpose(bank[4][:, c * P:(c + 1) * P], on[r % 2][:, c * P:(c + 1) * P], ident[:, :])
                last.then_inc(sem(sm("at_done")), 1)

            def moe_transposes(k):
                if k is None:
                    return
                b, r = k
                pe.wait_ge(sem(sm("xn2_done")), b + 1)
                pe.wait_ge(sem(sm("qk_out")), ahead(b, 4))
                wait(pe, sm("silu_done"), b)
                for c in range(KC):
                    last = nc.tensor.transpose(bank[5][:, c * P:(c + 1) * P], pay[r][:, c * P:(c + 1) * P], ident[:, :])
                last.then_inc(sem(sm("t2_done")), 1)

            def moe_up(k):
                if k is None:
                    return
                b, r = k
                p = r % 2
                pe.wait_ge(sem(sm("x2t_out")), b + 1)
                pe.wait_ge(sem(sm("at_out")), ahead(b, 2))
                wait(pe, sm("xa_done"), b)
                for c in range(KC):
                    last = nc.tensor.matmul(bank[4][:, 256:256 + E], x2t[p][:, c, :], w_gate[:, c, :],
                                            start=(c == 0), stop=(c == KC - 1))
                last.then_inc(sem(sm("logits_done")), 1)
                for n, w in enumerate((w_sg, w_su)):
                    for j in range(FS // P):
                        for c in range(KC):
                            last = nc.tensor.matmul(bank[5][:, n * FS + j * P:n * FS + (j + 1) * P],
                                                    w[:, c, j * P:(j + 1) * P], x2t[p][:, c, :],
                                                    start=(c == 0), stop=(c == KC - 1))
                last.then_inc(sem(sm("up_done")), 1)

            def moe_down(k):
                if k is None:
                    return
                b, r = k
                pe.wait_ge(sem(sm("silu_done")), b + 1)
                pe.wait_ge(sem(sm("xt_out")), ahead(b, 5))
                pe.wait_ge(sem(sm("en_out")), b + 1)
                pe.wait_ge(sem(sm("at_out")), ahead(b, 2))
                for c in range(FS // P):
                    last = nc.tensor.matmul(bank[4][:, 0:D], ht[r % 2][:, c, :], w_sd[:, c, :],
                                            start=(c == 0), stop=(c == FS // P - 1))
                last.then_inc(sem(sm("down_done")), 1)

            def moe_counts(k):
                if k is None:
                    return
                b, r = k
                pe.wait_ge(sem(sm("sel_done")), b + 1)
                pe.wait_ge(sem(sm("x3_done")), ahead(b, 2))
                pe.wait_ge(sem(sm("v_out")), ahead(b, 5))
                wait(pe, sm("pos_done"), b)
                nc.tensor.matmul(bank[6][:, D:D + E], strict_tri[:, :], sel[r % 2][:, :], start=True, stop=True)
                nc.tensor.matmul(bank[6][:, D + E:D + 2 * E], onesb[:, :], sel[r % 2][:, :], start=True,
                                 stop=True).then_inc(sem(sm("counts_done")), 1)

            def body(stage):
                f, m, k, o, w, v = (stage(lag) for lag in range(6))
                if L == 0:
                    probs_t(k, 3)
                    values(k, 2)
                    moe_up(w)
                transposes(f)
                if L == 0:
                    moe_counts(v)
                else:
                    probs_t(k, 3)
                    values(k, 2)
                output(o)
                if L == 0:
                    scores(m, 1)
                project_qk(f)
                if L == 0:
                    moe_down(w)
                else:
                    scores(m, 1)
                probs_t(m, 0)
                values(k, 3)
                scores(m, 2)
                project_v(f)
                heads_to_tokens(k)
                probs_t(m, 1)
                values(m, 0)
                scores(m, 3)
                tokens_to_heads(k)
                probs_t(m, 2)
                values(m, 1)
                if L == 0:
                    moe_transposes(o)
                scores(f, 0)

            attention_slots(pe, body)

        def attention_act(act, L):
            def sm(name):
                return f"{name}_{L}"

            def exponent(m, g):
                if m is None:
                    return
                b, _ = m
                act.wait_ge(sem(sm("max_done")), 4 * b + g + 1)
                wait(act, sm("pt_done"), 4 * b + g - 3)
                for h in range(GH):
                    last = nc.scalar.activation(sc[g][:, h, :], bank[g % 2][:, h * P:(h + 1) * P], ACT.Exp,
                                                bias=mx[:, GH * g + h:GH * g + h + 1])
                last.then_inc(sem(sm("exp_done")), 1)

            def copy_pt(m, g):
                if m is None:
                    return
                b, _ = m
                act.wait_ge(sem(sm("pt_done")), 4 * b + g + 1)
                wait(act, sm("pv_done"), 4 * b + g - 1)
                nc.scalar.copy(pt[g % 2][:, :, :], bank[2 + g % 2][:, :].rearrange("p (h q) -> p h q", h=GH)
                               ).then_inc(sem(sm("pt_out")), 1)

            def copy_xt(f):
                if f is None:
                    return
                b, r = f
                act.wait_ge(sem(sm("t_done")), b + 1)
                wait(act, sm("v_done"), b - 1)
                nc.scalar.copy(xt[r % 2][:, :, :], bank[4][:, 0:D].rearrange("p (c t) -> p c t", c=KC)
                               ).then_inc(sem(sm("xt_out")), 1)

            def copy_qk(f):
                if f is None:
                    return
                b, r = f
                p = r % 2
                act.wait_ge(sem(sm("qk_done")), b + 1)
                wait(act, sm("s_done"), 4 * (b - 1))
                wait(act, sm(f"kbd_in{p}"), 64 * (b - p))
                nc.scalar.copy(qk[p][:, :, :], bank[5][:, :].rearrange("p (c t) -> p c t", c=2 * KC)
                               ).then_inc(sem(sm("qk_out")), 1)

            def copy_v(f):
                if f is None:
                    return
                b, r = f
                act.wait_ge(sem(sm("v_done")), b + 1)
                wait(act, sm("pv_done"), 4 * (b - 1))
                nc.scalar.copy(vx[r % 2][:, :, 0:DH], bank[6][:, 0:D].rearrange("p (h d) -> p h d", h=H)
                               ).then_inc(sem(sm("v_out")), 1)

            def normalise(n, k):
                if n is None and k is None:
                    return
                s1 = n[0] if n is not None else k[0] + 4
                if k is not None:
                    b, r = k
                    act.wait_ge(sem(sm("rstd_step")), NORM_STEPS * (s1 + 1))
                    if L == 0:
                        wait(act, f"scattered{r}", 32 * (b - r))
                        dst = pay[r][:, 0:D]
                    else:
                        dst = xn3[:, bass.ds(b, 1), :].rearrange("p o d -> p (o d)")
                    hold(act)
                    nc.scalar.activation(dst, row(b), ACT.Identity, bias=nmr[:, 1:2], scale=rstd[:, 1:2]
                                         ).then_inc(sem(sm("xn2_done")), 1)
                if n is not None:
                    b, r = n
                    act.wait_ge(sem(sm("rstd_step")), NORM_STEPS * (s1 + 1))
                    wait(act, sm("t_done"), b - 1)
                    hold(act)
                    nc.scalar.activation(xn[r % 2][:, :], row(b), ACT.Identity, bias=nmr[:, 0:1], scale=rstd[:, 0:1]
                                         ).then_inc(sem(sm("xn1_done")), 1)

            def copy_ov(k):
                if k is None:
                    return
                b, r = k
                act.wait_ge(sem(sm("pv_done")), 4 * b + 4)
                wait(act, sm("ot_done"), b - 1)
                nc.scalar.copy(ov[r % 2][:, :, :], bank[7][:, :].rearrange("p (g q) -> p g q", g=NG)
                               ).then_inc(sem(sm("ov_out")), 1)

            def copy_at(k):
                if k is None:
                    return
                b, r = k
                act.wait_ge(sem(sm("at_done")), b + 1)
                wait(act, sm("o_done"), b - 1)
                nc.scalar.copy(at[r % 2][:, :, :], bank[4][:, 0:D].rearrange("p (c t) -> p c t", c=KC)
                               ).then_inc(sem(sm("at_out")), 1)

            def copy_x2t(k):
                if k is None:
                    return
                b, r = k
                act.wait_ge(sem(sm("t2_done")), b + 1)
                wait(act, sm("up_done"), b - 1)
                nc.scalar.copy(x2t[r % 2][:, :, :], bank[5][:, 0:D].rearrange("p (c t) -> p c t", c=KC)
                               ).then_inc(sem(sm("x2t_out")), 1)

            def router_exp(k):
                if k is None:
                    return
                b, r = k
                act.wait_ge(sem(sm("logits_done")), b + 1)
                wait(act, sm("sel_done"), b - 1)
                nc.scalar.activation(en[r % 2][:, :], bank[4][:, 256:256 + E], ACT.Exp, scale=-1.0
                                     ).then_inc(sem(sm("en_out")), 1)

            def gate_tanh(k):
                if k is None:
                    return
                b, r = k
                act.wait_ge(sem(sm("up_done")), b + 1)
                wait(act, sm("silu_done"), b - 1)
                nc.scalar.activation(th[r % 2][:, :], bank[5][:, 0:FS], ACT.Tanh, scale=0.5).then_inc(sem(sm("th_out")), 1)

            def body(stage):
                n, f, m, k, o, w = (stage(lag) for lag in range(-1, 5))
                if L == 1:
                    copy_xt(f)
                exponent(m, 0)
                copy_pt(k, 3)
                if L == 0:
                    router_exp(w)
                    gate_tanh(w)
                    copy_xt(f)
                copy_qk(f)
                exponent(m, 1)
                copy_ov(k)
                copy_pt(m, 0)
                exponent(m, 2)
                copy_pt(m, 1)
                copy_v(f)
                copy_at(k)
                normalise(n, o)
                exponent(m, 3)
                copy_pt(m, 2)
                if L == 0:
                    copy_x2t(o)

            attention_slots(act, body)

        def attention_dve(dve, L):
            def sm(name):
                return f"{name}_{L}"

            def maximum(m, g):
                if m is None:
                    return
                b, _ = m
                dve.wait_ge(sem(sm("s_done")), 4 * b + g + 1)
                nc.vector.tensor_reduce(mx[:, GH * g:GH * g + GH], bank[g % 2][:, :].rearrange("p (h k) -> p h k", h=GH),
                                        AX, ALU.max, negate=True).then_inc(sem(sm("max_done")), 1)

            def residual(k):
                if k is None:
                    return
                b, _ = k
                dve.wait_ge(sem(sm("o_done")), b + 1)
                hold(dve)
                nc.vector.scalar_tensor_tensor(row(b), bank[6][:, 0:D], tg[:, L:L + 1], row(b), ALU.mult, ALU.add
                                               ).then_inc(sem(sm("x3_done")), 1)

            def second_stats(k):
                if k is None:
                    return
                b, _ = k
                dve.wait_ge(sem(sm("x3_done")), b + 1)
                hold(dve)
                nc.vector.bn_stats(st2[:, :], row(b)).then_inc(sem(sm("st2_done")), 1)

            def first_sum(n):
                if n is None or L == 0:
                    return
                b, r = n
                p = r % 2
                dve.wait_ge(sem(f"ax_in{p}"), 16 * (b - p) + 32)
                hold(dve)
                nc.vector.tensor_tensor(row(b), ax[p][:, 0, :], ax[p][:, 1, :], ALU.add).then_inc(sem(sm("sum_done")), 1)

            def first_stats(n):
                if n is None:
                    return
                b, r = n
                if L == 0:
                    dve.wait_ge(sem(sm(f"tile_in{r}")), 8 * (b - r) + 32)
                else:
                    dve.wait_ge(sem(sm("sum_done")), b + 1)
                hold(dve)
                nc.vector.bn_stats(st1[:, :], row(b)).then_inc(sem(sm("st1_done")), 1)

            def variances(n, k):
                last = None
                if k is not None:
                    dve.wait_ge(sem(sm("st2_done")), k[0] + 1)
                    hold(dve)
                    last = nc.vector.bn_aggr(mv[:, 1, :], st2[:, :])
                if n is not None:
                    dve.wait_ge(sem(sm("st1_done")), n[0] + 1)
                    hold(dve)
                    last = nc.vector.bn_aggr(mv[:, 0, :], st1[:, :])
                if last is not None:
                    last.then_inc(sem(sm("stats_done")), 1)

            def inverses(n, k):
                if n is None and k is None:
                    return
                s1 = n[0] if n is not None else k[0] + 4
                V = nc.vector
                st = Steps(dve, sm("rstd_step"), NORM_STEPS, s1)
                dve.wait_ge(sem(sm("stats_done")), s1 + 1)
                st.mark(V.tensor_scalar(var[:, :], mv[:, :, 1], EPS, None, ALU.add))
                yield
                st.need()
                st.mark(V.tensor_scalar(root[:, :].bitcast(i32), var[:, :].bitcast(i32), 1, None, ALU.arith_shift_right))
                yield
                st.need()
                st.mark(V.tensor_scalar(root[:, :].bitcast(i32), root[:, :].bitcast(i32), -1.0, float(0x5f3759df), ALU.mult, ALU.add))
                for step in range(3):
                    yield
                    st.need()
                    st.mark(V.scalar_tensor_tensor(newton[:, :], root[:, :], -0.5, root[:, :], ALU.mult, ALU.mult))
                    yield
                    st.need()
                    st.mark(V.tensor_tensor(newton[:, :], newton[:, :], var[:, :], ALU.mult))
                    yield
                    st.need()
                    if step == 2:
                        wait(dve, sm("xn1_done"), min(s1, NB) if isinstance(s1, int) else s1)
                        wait(dve, sm("xn2_done"), s1 - 4)
                    st.mark(V.scalar_tensor_tensor((rstd if step == 2 else root)[:, :], newton[:, :], 1.5, root[:, :],
                                                   ALU.add, ALU.mult))
                yield
                st.need()
                st.mark(V.scalar_tensor_tensor(nmr[:, :], mv[:, :, 0], -1.0, rstd[:, :], ALU.mult, ALU.mult))
                st.end()

            def token_maximum(k):
                if k is None or L == 0:
                    return
                b, _ = k
                dve.wait_ge(sem(sm("xn2_done")), b + 1)
                hold(dve)
                nc.vector.tensor_reduce(tmax[:, bass.ds(b, 1)], xn3[:, bass.ds(b, 1), :].rearrange("p o d -> p (o d)"), AX,
                                        ALU.max, apply_absolute_value=True).then_inc(sem("tmax_done"), 1)

            def head_sums(k):
                if k is None:
                    return
                b, r = k
                dve.wait_ge(sem(sm("ot_done")), b + 1)
                nc.vector.reciprocal(rden[:, :, :], bank[4][:, :].rearrange("p (h e) -> p h e", e=32)[:, :, DH:DH + 1]
                                     ).then_inc(sem(sm("rden_done")), 1)

            def head_norm(k):
                if k is None:
                    return
                b, r = k
                dve.wait_ge(sem(sm("rden_done")), b + 1)
                wait(dve, sm("at_done"), b - 1)
                nc.vector.tensor_tensor(on[r % 2][:, :].rearrange("p (h d) -> p h d", h=H),
                                        bank[4][:, :].rearrange("p (h e) -> p h e", e=32)[:, :, 0:DH],
                                        rden[:, :, :].broadcast_to([P, H, DH]), ALU.mult).then_inc(sem(sm("on_done")), 1)

            def silu(k):
                if k is None:
                    return
                b, r = k
                dve.wait_ge(sem(sm("th_out")), b + 1)
                nc.vector.scalar_tensor_tensor(hs[:, :], th[r % 2][:, :], 1.0, bank[5][:, 0:FS], ALU.add, ALU.mult
                                               ).then_inc(sem(sm("hs_done")), 1)

            def silu_up(k):
                if k is None:
                    return
                b, r = k
                dve.wait_ge(sem(sm("hs_done")), b + 1)
                wait(dve, sm("down_done"), b - 1)
                nc.vector.tensor_tensor(ht[r % 2][:, :, :].rearrange("p c t -> p (c t)"), hs[:, :], bank[5][:, FS:2 * FS],
                                        ALU.mult).then_inc(sem(sm("silu_done")), 1)

            def shared_out(k):
                if k is None:
                    return
                b, r = k
                p = r % 2
                dve.wait_ge(sem(sm("down_done")), b + 1)
                wait(dve, f"xa_stored{p}", 8 * (b - p))
                hold(dve)
                nc.vector.scalar_tensor_tensor(xa[p][:, :], bank[4][:, 0:D], tg_half[:, 0:1], row(b), ALU.mult,
                                               ALU.add).then_inc(sem(sm("xa_done")), 1)

            def route(k):
                if k is None:
                    return
                b, r = k
                st = Steps(dve, sm("route_step"), 16, b)
                V = nc.vector
                dve.wait_ge(sem(sm("en_out")), b + 1)
                st.mark(V.tensor_scalar(score[:, :], en[r % 2][:, :], 1.0, None, ALU.add))
                yield
                st.need()
                st.mark(V.reciprocal(score[:, :], score[:, :]))
                yield
                st.need()
                st.mark(V.tensor_tensor(sfc[:, :], score[:, :], ebias[:, :], ALU.add))
                yield
                st.need()
                hold(dve)
                for g in range(EG):
                    last = V.max(m8[:, g, :], sfc[:, g * EPG:(g + 1) * EPG])
                st.mark(last)
                yield
                st.need()
                st.mark(V.tensor_tensor(gs[:, 0:EG], m8[:, :, 0], m8[:, :, 1], ALU.add))
                yield
                st.need()
                hold(dve)
                st.mark(V.max(top[:, :], gs[:, 0:EG]))
                yield
                st.need()
                st.mark(V.tensor_copy(tog[:, 0:GSEL], top[:, 0:GSEL]))
                yield
                st.need()
                hold(dve)
                st.mark(V.match_replace(grep[:, :], tog[:, :], gs[:, :], -LOW))
                yield
                st.need()
                st.mark(V.tensor_scalar(gmask[:, :, 0], grep[:, 0:EG], -LOW, None, ALU.is_ge))
                yield
                st.need()
                st.mark(V.tensor_tensor(tmp[:, :].rearrange("p (g e) -> p g e", g=EG),
                                        sfc[:, :].rearrange("p (g e) -> p g e", g=EG),
                                        gmask[:, :, :].broadcast_to([P, EG, EPG]), ALU.mult))
                yield
                st.need()
                st.mark(V.tensor_scalar(tmp[:, :], tmp[:, :], 0.0, None, ALU.add))
                yield
                st.need()
                hold(dve)
                st.mark(V.max(top[:, :], tmp[:, :]))
                yield
                st.need()
                hold(dve)
                st.mark(V.match_replace(rep[:, :], top[:, :], tmp[:, :], LOW))
                yield
                st.need()
                wait(dve, sm("counts_done"), b - 1)
                V.tensor_scalar(sel[r % 2][:, :], rep[:, :], LOW, None, ALU.is_le).then_inc(sem(sm("sel_done")), 1)
                V.tensor_scalar(self_[:, :], rep[:, :], LOW, None, ALU.is_le)
                st.mark(V.scalar_tensor_tensor(wun[:, :], rep[:, :], LOW, score[:, :], ALU.is_le, ALU.mult,
                                               accum_out=wsum[:, 0:1]))
                yield
                st.need()
                st.mark(V.tensor_scalar(wsum[:, :], wsum[:, :], 1e-20, None, ALU.add))
                yield
                st.need()
                st.mark(V.reciprocal(wsum[:, :], wsum[:, :]))
                yield
                st.need()
                V.tensor_scalar(pay[r][:, D:D + E], wun[:, :], wsum[:, 0:1], tg_route[:, 0:1], ALU.mult, ALU.mult)
                V.tensor_scalar(pay[r][:, TOKC:TOKC + 1], pay[r][:, TOKC:TOKC + 1], 4.0 * P, None, ALU.add)
                st.end()

            def dispatch(k):
                if k is None:
                    return
                b, r = k
                st = Steps(dve, sm("slot_step"), 6, b)
                V = nc.vector
                dve.wait_ge(sem(sm("counts_done")), b + 1)
                st.mark(V.tensor_tensor(pos[:, :], bank[6][:, D:D + E], count[:, :], ALU.add))
                yield
                st.need()
                V.tensor_tensor(count[:, :], bank[6][:, D + E:D + 2 * E], count[:, :], ALU.add).then_inc(sem(sm("pos_done")), 1)
                V.tensor_tensor(key[:, :], pos[:, :], slot_base[:, :], ALU.add)
                st.mark(V.scalar_tensor_tensor(valid[:, :], pos[:, :], float(CAP), self_[:, :], ALU.is_lt, ALU.mult))
                yield
                st.need()
                st.mark(V.tensor_tensor(key[:, :], key[:, :], valid[:, :], ALU.mult))
                yield
                st.need()
                hold(dve)
                st.mark(V.max(keys8[:, :], key[:, :]))
                yield
                st.need()
                st.mark(V.tensor_scalar(far[:, :], keys8[:, :], 0.0, float(1 << 20), ALU.is_equal, ALU.mult))
                yield
                st.need()
                wait(dve, f"scattered{r}", 32 * (b - r))
                st.mark(V.scalar_tensor_tensor(idx[r][:, :], keys8[:, :], -1.0, far[:, :], ALU.add, ALU.add))
                st.end()

            def body(stage):
                n, f, m, k, o, w, v = (stage(lag) for lag in range(-1, 6))
                r, d = route(w if L == 0 else None), dispatch(v if L == 0 else None)

                q = inverses(n, o)

                def routing(steps):
                    for _ in range(steps):
                        next(r, None)

                def norming(steps):
                    for _ in range(steps):
                        next(q, None)
                        next(r, None)

                def dispatching():
                    next(d, None)

                maximum(m, 0)
                first_sum(n)
                routing(1)
                first_stats(n)
                routing(1)
                if L == 0:
                    silu(w)
                routing(1)
                if L == 0:
                    silu_up(w)
                residual(o)
                dispatching()
                second_stats(o)
                dispatching()
                variances(n, o)
                dispatching()
                maximum(m, 1)
                dispatching()
                dispatching()
                norming(1)
                dispatching()
                norming(5)
                if L == 0:
                    shared_out(w)
                norming(2)
                maximum(m, 2)
                norming(2)
                head_sums(k)
                norming(1)
                head_norm(k)
                norming(2)
                maximum(m, 3)
                token_maximum(o)
                routing(17)
            attention_slots(dve, body)

        def attention_sp(sp, L):
            def sm(name):
                return f"{name}_{L}"

            ctx_v = a["ctx_1024"]

            def load(n):
                if n is None:
                    return
                b, r = n
                p = r % 2
                wait(sp, sm("v_done"), b - 3)
                hold(sp)
                sp.dma_start(cx[r][:, :, :], ctx_v[bass.ds(b, 1), :, :].rearrange("o (k p) s -> p (o k) s", p=P)
                             ).then_inc(sem(sm(f"tile_in{r}")), 16)
                if L == 0:
                    sp.dma_start(res[:, bass.ds(b, 1), :].rearrange("p o d -> p (o d)"),
                                 a["x"][bass.ds(b, 1), :, :].rearrange("o p d -> p (o d)")).then_inc(sem(sm(f"tile_in{r}")), 16)
                else:
                    wait(sp, sm("sum_done"), b - 1)
                    hold(sp)
                    for n_ in range(2):
                        sp.dma_start(ax[p][:, n_, :], acc[n_][bass.ds(b * P, P), :]).then_inc(sem(f"ax_in{p}"), 16)

            def spread(f):
                if f is None:
                    return
                b, r = f
                p = r % 2
                sp.wait_ge(sem(sm("qk_out")), b + 1)
                hold(sp)
                for h in range(HB):
                    sp.dma_start(kbd[p][DH * h:DH * (h + 1), :, h * P:(h + 1) * P],
                                 qk[p][DH * h:DH * (h + 1), KC:2 * KC, :]).then_inc(sem(sm(f"kbd_in{p}")), 16)

            def store(k):
                if k is None:
                    return
                b, r = k
                sp.wait_ge(sem(sm("xa_done")), b + 1)
                hold(sp)
                sp.dma_start(acc[0][bass.ds(b * P, P), :], xa[r % 2][:, :]).then_inc(sem(f"xa_stored{r % 2}"), 16)
                sp.dma_start(acc[1][bass.ds(b * P, P), :], zt[:, 0, 0:D]).then_inc(sem("acc_zero"), 16)

            def body(stage):
                load(stage(-2))
                spread(stage(0))
                if L == 0:
                    store(stage(4))

            load((0, 0))
            attention_slots(sp, body)

        def expert_slots(eng, body):
            slots(eng, body, E, 4, 4 + (E - 5) // 4 * 4, 0, E + 2, 4)

        def experts_sp(sp):
            xe_v = xe.rearrange("(e h p) c -> e p h c", p=P, h=HALVES)

            def load_rows(e):
                if e is None:
                    return
                b, r = e
                wait(sp, "e_t_done", b - 3)
                wait(sp, "e_w_done", b - 3)
                hold(sp)
                sp.dma_start(xr[r][:, :, :], xe_v[bass.ds(b, 1)].rearrange("o p h c -> p (o h) c")
                             ).then_inc(sem(f"e_rows_in{r}"), 16)

            def load_weights(e):
                if e is None:
                    return
                b, r = e
                wait(sp, "e_up_done", b - 3)
                wait(sp, "e_down_done", b - 3)
                hold(sp)
                one = bass.ds(b, 1)
                sp.dma_start(wa[r], a["L0_ffn_w1"][one].rearrange("o (k p) f -> p (o k) f", p=P)).then_inc(sem(f"e_w_in{r}"), 16)
                sp.dma_start(wb[r], a["L0_ffn_w3"][one].rearrange("o (k p) f -> p (o k) f", p=P)).then_inc(sem(f"e_w_in{r}"), 16)
                sp.dma_start(wc[r], a["L0_ffn_w2"][one].rearrange("o f d -> f (o d)")).then_inc(sem(f"e_w_in{r}"), 16)

            def body(stage):
                e = stage(0)
                load_rows(stage(-1))
                load_weights(e)
                if e is not None and isinstance(e[0], int) and e[0] == 3:
                    attention_weights(sp, 1, "w_in")

            load_rows((0, 0))
            expert_slots(sp, body)

        def experts_pe(pe):
            def rows_t(e):
                if e is None:
                    return
                b, r = e
                p = r % 2
                pe.wait_ge(sem(f"e_rows_in{r}"), 4 * (b - r) + 16)
                wait(pe, "e_xt_out", b - 1)
                for c in range(KC):
                    for h in range(HALVES):
                        last = nc.tensor.transpose(bank[p][:, c * CAP + h * P:c * CAP + (h + 1) * P],
                                                   xr[r][:, h, c * P:(c + 1) * P], ident[:, :])
                last.then_inc(sem("e_t_done"), 1)

            def up(e):
                if e is None:
                    return
                b, r = e
                p = r % 2
                pe.wait_ge(sem("e_xt_out"), b + 1)
                pe.wait_ge(sem(f"e_w_in{r}"), 12 * (b - r) + 48)
                wait(pe, "e_h_done", b - 1)
                for n, w in enumerate((wa, wb)):
                    for c in range(KC):
                        last = nc.tensor.matmul(bank[2 + p][:, n * CAP:(n + 1) * CAP], w[r][:, c, :], xrt[p][:, c, :],
                                                start=(c == 0), stop=(c == KC - 1))
                last.then_inc(sem("e_up_done"), 1)

            def down(e):
                if e is None:
                    return
                b, r = e
                p = r % 2
                pe.wait_ge(sem("e_h_done"), b + 1)
                wait(pe, "e_y_done", b - 1)
                for h in range(HALVES):
                    last = nc.tensor.matmul(bank[4 + p][:, h * D:(h + 1) * D], he[p][:, h * P:(h + 1) * P], wc[r],
                                            start=True, stop=True)
                last.then_inc(sem("e_down_done"), 1)

            def body(stage):
                rows_t(stage(0))
                up(stage(1))
                down(stage(2))

            expert_slots(pe, body)

        def experts_act(act):
            def copy_t(e):
                if e is None:
                    return
                b, r = e
                act.wait_ge(sem("e_t_done"), b + 1)
                wait(act, "e_up_done", b - 1)
                nc.scalar.copy(xrt[r % 2][:, :, :], bank[r % 2][:, :].rearrange("p (c t) -> p c t", c=KC)).then_inc(sem("e_xt_out"), 1)

            def silu(e):
                if e is None:
                    return
                b, r = e
                act.wait_ge(sem("e_up_done"), b + 1)
                wait(act, "e_h_done", b - 1)
                nc.scalar.activation(sg[r % 2][:, :], bank[2 + r % 2][:, 0:CAP], ACT.Silu).then_inc(sem("e_sg_done"), 1)

            def body(stage):
                copy_t(stage(0))
                silu(stage(1))

            expert_slots(act, body)

        def experts_dve(dve):
            def weights(e):
                if e is None:
                    return
                b, r = e
                p = r % 2
                dve.wait_ge(sem(f"e_rows_in{r}"), 4 * (b - r) + 16)
                wait(dve, "e_y_done", b - 3)
                wait(dve, f"e_added{p}", 16 * (b - p - 2))
                nc.vector.tensor_copy(wcol[r][:, :].unsqueeze(2), xr[r][:, :, bass.ds(b + D, 1)])
                nc.vector.tensor_copy(tid[r][:, :], xr[r][:, :, TOKC]).then_inc(sem("e_w_done"), 1)

            def hidden(e):
                if e is None:
                    return
                b, r = e
                p = r % 2
                dve.wait_ge(sem("e_sg_done"), b + 1)
                wait(dve, "e_down_done", b - 1)
                nc.vector.tensor_tensor(he[p][:, :], sg[p][:, :], bank[2 + p][:, CAP:2 * CAP], ALU.mult).then_inc(sem("e_h_done"), 1)

            def outputs(e):
                if e is None:
                    return
                b, r = e
                p = r % 2
                dve.wait_ge(sem("e_down_done"), b + 1)
                dve.wait_ge(sem("e_w_done"), b + 1)
                for h in range(HALVES):
                    last = nc.vector.tensor_scalar(ye[r][:, h, :], bank[4 + p][:, h * D:(h + 1) * D], wcol[r][:, h:h + 1], None, ALU.mult)
                last.then_inc(sem("e_y_done"), 1)

            def body(stage):
                outputs(stage(2))
                weights(stage(0))
                hidden(stage(1))

            expert_slots(dve, body)

        def experts_pool(pool):
            def add(e):
                if e is None:
                    return
                b, r = e
                p = r % 2
                pool.wait_ge(sem("e_y_done"), b + 1)
                wait(pool, f"e_added{p}", 16 * (b - p))
                hold(pool)
                for h in range(HALVES):
                    nc.gpsimd.indirect_dma_start(
                        out=acc[p][:, :], out_offset=bass.IndirectOffsetOnAxis(ap=tid[r][:, h:h + 1], axis=0),
                        in_=ye[r][:, h, :], in_offset=None, bounds_check=T + HALVES * P - 1, oob_is_err=True,
                        compute_op=ALU.add).then_inc(sem(f"e_added{p}"), 16)

            expert_slots(pool, lambda stage: add(stage(2)))
            for p in range(2):
                pool.wait_ge(sem(f"e_added{p}"), 16 * E)

        assert IC == 6 and TPC == 4
        GUB = 3

        def weights_dve(dve):
            V = nc.vector
            st = Steps(dve, "wq_step", 8 * 2 + 8, 0)
            dve.wait_ge(sem("ffn_w_in"), 16 * (5 if IREST else 3))
            for n in range(2):
                st.then(V.tensor_reduce(s_gu[:, n, 0:IC], wraw[n], AX, ALU.max, apply_absolute_value=True))
                st.then(V.tensor_scalar(s_gu[:, n, :], s_gu[:, n, :], 1.0 / QMAX, None, ALU.mult))
                if IREST:
                    st.then(V.tensor_scalar(inv[:, 0:1], s_gu[:, n, 0:1], 1.0, None, ALU.mult))
                    st.then(V.memset(s_gu[IREST:P, n, IC - 1:IC], 1.0))
                st.then(V.reciprocal(inv[:, n * IC:(n + 1) * IC], s_gu[:, n, :]))
                st.then(V.tensor_tensor(wraw[n], wraw[n], inv[:, n * IC:(n + 1) * IC].unsqueeze(2).broadcast_to([P, IC, D]), ALU.mult))
                st.then(V.tensor_scalar(wraw[n], wraw[n], RND, -RND, ALU.add, ALU.add))
                if n == 1:
                    dve.wait_ge(sem("w_t_out"), 1)
                st.then(V.tensor_scalar(wq_b[:, 0:IC * D].rearrange("p (c d) -> p c d", c=IC), wraw[n], QMAX, -QMAX - 1.0, ALU.min, ALU.max))
                dve.sem_inc(sem("w_int"), 1)
            st.then(V.tensor_reduce(s_d[:, :], wdraw[:, :, :], AX, ALU.max, apply_absolute_value=True))
            st.then(V.tensor_scalar(s_d[:, :], s_d[:, :], 1.0 / QMAX, None, ALU.mult))
            st.then(V.reciprocal(inv[:, 2 * IC:2 * IC + KC], s_d[:, :]))
            st.then(V.tensor_tensor(wdraw[:, :, :], wdraw[:, :, :], inv[:, 2 * IC:2 * IC + KC].unsqueeze(2).broadcast_to([P, KC, I]), ALU.mult))
            st.then(V.tensor_scalar(wdraw[:, :, :], wdraw[:, :, :], RND, -RND, ALU.add, ALU.add))
            dve.wait_ge(sem("w_t_out"), 2)
            wd_b = wq_b[:, :].rearrange("p (c i) -> p c i", c=KC)
            st.then(V.memset(wd_b[:, :, I:IP], 0.0)) if IP > I else st.then(V.memset(inv[:, 0:1], 0.0))
            st.then(V.tensor_scalar(wd_b[:, :, 0:I], wdraw[:, :, :], QMAX, -QMAX - 1.0, ALU.min, ALU.max))
            dve.sem_inc(sem("w_int"), 1)
            dve.wait_ge(sem("gmax_done"), 1)
            dve.wait_ge(sem("sig_done"), 1)
            st.then(V.tensor_scalar(sig[:, :], sig[:, :], 1.0, None, ALU.add))
            st.end()
            st = Steps(dve, "sx_step", 4, 0)
            st.then(V.reciprocal(sig[:, :], sig[:, :]))
            st.then(V.tensor_scalar(scl[:, 0:1], gmax[:, 0:1], sig[:, 0:1], 1.0 / QMAX, ALU.mult, ALU.mult))
            st.then(V.reciprocal(scl[:, 1:2], scl[:, 0:1]))
            st.then(V.tensor_scalar(s_gux[:, :, :], s_gu[:, :, :], scl[:, 0:1], None, ALU.mult))
            dve.sem_inc(sem("sx_done"), 1)
            st.end()

        def weights_pe(pe):
            bb = [bank[k][:, :].bitcast(bf16) for k in range(3)]
            for n in range(3):
                pe.wait_ge(sem("w_int"), n + 1)
                for half in range(2):
                    if n or half:
                        pe.wait_ge(sem("w_half_out"), 2 * n + half)
                    for c in range(IC):
                        if n < 2:
                            src = wq_b[:, c * D + half * P:c * D + (half + 1) * P]
                        else:
                            src = wq_b[:, half * IP + c * P:half * IP + (c + 1) * P]
                        last = nc.tensor.transpose(bb[0][:, c * P:(c + 1) * P], src, identb[:, :])
                    last.then_inc(sem("w_half_t"), 1)
            pe.wait_ge(sem("sd_wide"), 1)
            for c in range(KC):
                last = nc.tensor.transpose(bank[1][:, c * P:(c + 1) * P], xq_f[0][:, c * P:(c + 1) * P], ident[:, :])
            last.then_inc(sem("sd_t"), 1)

        def weights_act(act):
            bb = bank[0][:, :].bitcast(bf16)
            for n in range(3):
                for half in range(2):
                    act.wait_ge(sem("w_half_t"), 2 * n + half + 1)
                    src = bb[:, 0:IC * P]
                    if n < 2:
                        last = nc.scalar.copy((wgi, wui)[n][:, half, :], src)
                    else:
                        last = nc.scalar.copy(wdi[:, :, half * P:(half + 1) * P], src.rearrange("p (c i) -> p c i", c=IC))
                    last.then_inc(sem("w_half_out"), 1)
                act.drain().then_inc(sem("w_t_out"), 1)

        def ffn_chunks(eng, body):
            slots(eng, body, NC_, 4, 4 + max(0, (NC_ - 4) // 4 * 4), 0, NC_ + 2, 4)

        def gate_up(pe, c, i, pas):
            if c is None:
                return
            b, r = c
            if i == 0 and not pas:
                pe.wait_ge(sem("xqt_out"), b + 1)
            g, u = bank[2 * (i % GUB)], bank[2 * (i % GUB) + 1]
            wait(pe, f"f_h{pas}", IC * b + i - GUB + 1)
            for k in range(KC):
                nc.tensor.matmul(g[:, :], wgi[:, k, i * P:(i + 1) * P], xqt[:, k, bass.ds(b * CT, CT)],
                                 start=(k == 0), stop=(k == KC - 1))
            for k in range(KC):
                last = nc.tensor.matmul(u[:, :], wui[:, k, i * P:(i + 1) * P], xqt[:, k, bass.ds(b * CT, CT)],
                                        start=(k == 0), stop=(k == KC - 1))
            last.then_inc(sem(f"f_gu_done{pas}"), 1)

        def silu_gate(act, c, i, pas):
            if c is None:
                return
            b, r = c
            act.wait_ge(sem(f"f_gu_done{pas}"), IC * b + i + 1)
            wait(act, f"f_h{pas}", IC * b + i - 2)
            nc.scalar.activation(f_sg[i % 3][:, :], bank[2 * (i % GUB)][:, :], ACT.Silu,
                                 scale=s_gux[:, 0, i:i + 1]).then_inc(sem(f"f_sg_done{pas}"), 1)

        def hidden(dve, c, i, pas, scale):
            if c is None:
                return
            b, r = c
            dve.wait_ge(sem(f"f_sg_done{pas}"), IC * b + i + 1)
            if pas and i % 2:
                wait(dve, "f_odd_done", IC // 2 * (b - 1) + i // 2 + 1)
            nc.vector.scalar_tensor_tensor(f_h[i][:, :], bank[2 * (i % GUB) + 1][:, :], scale[:, i:i + 1],
                                           f_sg[i % 3][:, :], ALU.mult, ALU.mult).then_inc(sem(f"f_h{pas}"), 1)

        def pass0_pe(pe):
            def xq_t(c):
                if c is None:
                    return
                b, r = c
                pe.wait_ge(sem("xq_done"), b + 1)
                wait(pe, "xqt_out", b)
                bb = bank[6][:, :].bitcast(bf16)
                for k in range(KC):
                    for t in range(TPC):
                        last = nc.tensor.transpose(bb[:, k * CT + t * P:k * CT + (t + 1) * P],
                                                   xq_b[r % 2][:, t, k * P:(k + 1) * P], identb[:, :])
                last.then_inc(sem("xq_t"), 1)

            def body(stage):
                for i in range(IC):
                    gate_up(pe, stage(2), i, 0)
                    if i == 2:
                        xq_t(stage(1))
            ffn_chunks(pe, body)

        def pass0_act(act):
            def convert(c):
                if c is None:
                    return
                b, r = c
                act.wait_ge(sem("xq_clipped"), b + 1)
                wait(act, "xq_t", b - 1)
                nc.scalar.activation(xq_b[r % 2][:, :, :].rearrange("p t d -> p (t d)"), xq_f[r % 2][:, :], ACT.Copy,
                                     bias=-RND).then_inc(sem("xq_done"), 1)

            def copy_t(c):
                if c is None:
                    return
                b, r = c
                act.wait_ge(sem("xq_t"), b + 1)
                hold(act)
                nc.scalar.copy(xqt[:, :, bass.ds(b * CT, CT)], bank[6][:, :].bitcast(bf16).rearrange("p (k t) -> p k t", k=KC)
                               ).then_inc(sem("xqt_out"), 1)

            def body(stage):
                for i in range(IC):
                    silu_gate(act, stage(2), i, 0)
                    if i == 0:
                        convert(stage(1))
                    if i == 4:
                        copy_t(stage(1))
            ffn_chunks(act, body)

        def pass0_pool(pool):
            def clip_tokens(c):
                if c is None:
                    return
                b, r = c
                pool.wait_ge(sem("xq_rounded"), b + 1)
                hold(pool)
                nc.gpsimd.tensor_scalar(xq_f[r % 2][:, :], xq_f[r % 2][:, :], RND + QMAX, RND - QMAX - 1.0, ALU.min, ALU.max
                                        ).then_inc(sem("xq_clipped"), 1)

            ffn_chunks(pool, lambda stage: clip_tokens(stage(0)))

        def pass0_dve(dve):
            V = nc.vector

            def quantise(c):
                if c is None:
                    return
                b, r = c
                wait(dve, "xq_done", b - 1)
                hold(dve)
                V.tensor_scalar(xq_f[r % 2][:, :], big[:, bass.ds(b * (TPC * D), TPC * D)], scl[:, 1:2], RND, ALU.mult,
                                ALU.add).then_inc(sem("xq_rounded"), 1)

            def maximum(c, i):
                if c is None:
                    return
                b, r = c
                dve.wait_ge(sem("f_h0"), IC * b + i + 1)
                hold(dve)
                V.tensor_reduce(hmax[:, bass.ds(b * IC + i, 1)], f_h[i][:, :], AX, ALU.max,
                                apply_absolute_value=True).then_inc(sem("f_max_done"), 1)

            def body(stage):
                quantise(stage(0))
                for i in range(IC + 1):
                    if i < IC:
                        hidden(dve, stage(2), i, 0, s_gux[:, 1, :])
                    if i >= 1:
                        maximum(stage(2), i - 1)
            ffn_chunks(dve, body)

        def pass1_pe(pe):
            def down(c, t):
                if c is None:
                    return
                b, r = c
                pe.wait_ge(sem("f_even_done"), (IC + 1) // 2 * (b + 1))
                pe.wait_ge(sem("f_odd_done"), IC // 2 * (b + 1))
                wait(pe, "f_y_read", TPC * b + t - 1)
                for i in range(IC):
                    last = nc.tensor.matmul(bank[6 + t % 2][:, 0:D], f_q[r % 2][:, i, t * P:(t + 1) * P], wdi[:, i, :],
                                            start=(i == 0), stop=(i == IC - 1))
                last.then_inc(sem("f_down_done"), 1)

            def body(stage):
                for i in range(IC):
                    gate_up(pe, stage(0), i, 1)
                    if i == 0:
                        down(stage(2), 3)
                    if i >= 3:
                        down(stage(1), i - 3)
            ffn_chunks(pe, body)

        def pass1_act(act):
            def offset(c, i):
                if c is None or not i % 2:
                    return
                b, r = c
                act.wait_ge(sem("f_clip_done"), IC * b + i + 1)
                nc.scalar.activation(f_h[i][:, :], f_h[i][:, :], ACT.Copy, bias=RND).then_inc(sem("f_offset_done"), 1)

            def integer(c, i):
                if c is None or not i % 2:
                    return
                b, r = c
                act.wait_ge(sem("f_offset_done"), IC // 2 * b + i // 2 + 1)
                if i == 1:
                    wait(act, "f_down_done", TPC * (b - 1))
                nc.scalar.activation(f_q[r % 2][:, i, :], f_h[i][:, :], ACT.Copy, bias=-RND).then_inc(sem("f_odd_done"), 1)

            def body(stage):
                for i in range(IC):
                    silu_gate(act, stage(0), i, 1)
                    if i >= 3:
                        offset(stage(0), i - 2)
                        integer(stage(0), i - 3)
                    if i == 0:
                        offset(stage(1), IC - 1)
                        integer(stage(1), IC - 3)
                    if i == 1:
                        integer(stage(1), IC - 1)
            ffn_chunks(act, body)

        def pass1_dve(dve):
            V = nc.vector

            def clip(c, i):
                if c is None:
                    return
                b, r = c
                dve.wait_ge(sem("f_h1"), IC * b + i + 1)
                V.tensor_scalar(f_h[i][:, :], f_h[i][:, :], QMAX, -QMAX - 1.0, ALU.min, ALU.max
                                ).then_inc(sem("f_clip_done"), 1)

            def rounded(c, i):
                if c is None or i % 2:
                    return
                b, r = c
                dve.wait_ge(sem("f_clip_done"), IC * b + i + 1)
                if i == 0:
                    wait(dve, "f_down_done", TPC * (b - 1))
                V.tensor_scalar(f_q[r % 2][:, i, :], f_h[i][:, :], RND, -RND, ALU.add, ALU.add).then_inc(sem("f_even_done"), 1)

            def scaled(c, t):
                if c is None:
                    return
                b, r = c
                dve.wait_ge(sem("f_down_done"), TPC * b + t + 1)
                wait(dve, f"f_stored{t}", 16 * b)
                V.tensor_tensor(yo[t], bank[6 + t % 2][:, 0:D], sd_row[:, :], ALU.mult).then_inc(sem("f_y_read"), 1)

            def body(stage):
                for i in range(IC):
                    hidden(dve, stage(0), i, 1, s_guq)
                    if i < 2:
                        scaled(stage(2), 2 + i)
                    if i >= 4:
                        scaled(stage(1), i - 4)
                    if i >= 1:
                        clip(stage(0), i - 1)
                    if i >= 2:
                        rounded(stage(0), i - 2)
                clip(stage(0), IC - 1)
                rounded(stage(0), IC - 2)
            ffn_chunks(dve, body)

        def pass1_pool(pool):
            def residual(c, t):
                if c is None:
                    return
                b, r = c
                pool.wait_ge(sem("f_y_read"), TPC * b + t + 1)
                hold(pool)
                nc.gpsimd.tensor_tensor(yo[t], yo[t], row(b * TPC + t), ALU.add).then_inc(sem("f_y_done"), 1)

            def body(stage):
                for t in (2, 3):
                    residual(stage(2), t)
                for t in (0, 1):
                    residual(stage(1), t)
            ffn_chunks(pool, body)

        def ffn_sp(sp):
            out_v = out.rearrange("b s d -> s b d")

            def store(c):
                if c is None:
                    return
                b, r = c
                for t in range(TPC):
                    sp.wait_ge(sem("f_y_done"), TPC * b + t + 1)
                    hold(sp)
                    sp.dma_start(out_v[:, bass.ds(b * TPC + t, 1), :].rearrange("s o d -> s (o d)"), yo[t]
                                 ).then_inc(sem(f"f_stored{t}"), 16)

            ffn_chunks(sp, lambda stage: store(stage(1)))
            for t in range(TPC):
                sp.wait_ge(sem(f"f_stored{t}"), 16 * NC_)

        def attention_weights(eng, L, name):
            n = (("L0_xattn_wq_w", "L0_xattn_wk_w", "L0_xattn_wv_w", "L0_xattn_wo_w"),
                 ("L1_xattn_wq", "L1_xattn_wk", "L1_xattn_wv", "L1_xattn_wo"))[L]
            v = (("L0_xattn_wq_b", "L0_xattn_wk_b", "L0_xattn_wv_b", "L0_xattn_wo_b"),
                 ("L1_xattn_bq", "L1_xattn_bk", "L1_xattn_bv", "L1_xattn_bo"))[L]
            for dst, src in zip((w_q, w_k, w_v, w_o), n):
                eng.dma_start(dst[:, :, :], a[src].rearrange("(k p) n -> p k n", p=P)).then_inc(sem(name), 16)
            for c, src in enumerate(v):
                eng.dma_start(bias[:, c * D:(c + 1) * D], a[src].unsqueeze(0).broadcast_to([P, D])).then_inc(sem(name), 16)

        def split_biases(dve, L):
            V = nc.vector
            st = Steps(dve, "bias_step", 9, L)
            V.tensor_scalar(w_q[:, :, :], w_q[:, :, :], SM_SCALE, None, ALU.mult)
            st.then(V.tensor_scalar(bias[:, 0:D], bias[:, 0:D], SM_SCALE, None, ALU.mult))
            st.then(V.tensor_copy(bias_part[:, :], bias[:, :]))
            st.then(V.tensor_scalar(bias3[:, :], bias_part[:, :], ident[:, 0:1], None, ALU.mult))
            for part in (1, 2):
                st.then(V.tensor_tensor(bias[:, :], bias[:, :], bias_part[:, :], ALU.subtract))
                st.then(V.tensor_copy(bias_part[:, :], bias[:, :]))
                st.then(V.scalar_tensor_tensor(bias3[:, :], bias_part[:, :], ident[:, part:part + 1], bias3[:, :],
                                               ALU.mult, ALU.add))
            st.end()

        block = ctx.enter_context(nc.Block())

        @block.sync
        def _(sp):
            attention_weights(sp, 0, "w_in")
            for n, g in enumerate(("g_xattn", "g_ffn")):
                sp.dma_start(gates[:, 2 * n:2 * n + 2], a[g].unsqueeze(0).broadcast_to([P, 2])).then_inc(sem("w_in"), 16)
            sp.dma_start(ebias[:, :], a["L0_ffn_e_bias"].unsqueeze(0).broadcast_to([P, E])).then_inc(sem("w_in"), 16)
            for dst, src in ((w_gate, "L0_ffn_gate_weight"), (w_sg, "L0_ffn_shared_gate"), (w_su, "L0_ffn_shared_up"),
                             (w_sd, "L0_ffn_shared_down")):
                sp.dma_start(dst[:, :, :], a[src].rearrange("(k p) n -> p k n", p=P)).then_inc(sem("w_in"), 16)
            sp.dma_start(mask_i[:, :], a["mask_1x1xSxS2_ik0"].rearrange("a b q k -> (a b q) k")).then_inc(sem("w_in"), 16)
            phase_end(sp, 1)
            attention_sp(sp, 0)
            for p in range(2):
                sp.wait_ge(sem(f"xa_stored{p}"), 8 * NB)
            sp.wait_ge(sem("acc_zero"), 16 * NB)
            phase_end(sp, 2)
            experts_sp(sp)
            phase_end(sp, 3)
            attention_sp(sp, 1)
            phase_end(sp, 4)
            for n, src in enumerate(("L1_ffn_w_gate", "L1_ffn_w_up")):
                sp.dma_start(wraw[n][:, 0:IFULL, :], a[src][0:IFULL * P, :].rearrange("(c p) d -> p c d", p=P)).then_inc(sem("ffn_w_in"), 16)
                if IREST:
                    sp.dma_start(wraw[n][0:IREST, IFULL, :], a[src][IFULL * P:I, :]).then_inc(sem("ffn_w_in"), 16)
            sp.dma_start(wdraw[:, :, :], a["L1_ffn_w_down"].rearrange("(k p) i -> p k i", p=P)).then_inc(sem("ffn_w_in"), 16)
            sp.dma_start(clips[:, 0:1], a["L1_ffn_clip_x"].unsqueeze(0).broadcast_to([P, 1])).then_inc(sem("clip_in"), 16)
            sp.dma_start(clips[:, 1:2], a["L1_ffn_clip_down"].unsqueeze(0).broadcast_to([P, 1])).then_inc(sem("clip_in"), 16)
            phase_end(sp, 5)
            phase_end(sp, 6)
            ffn_sp(sp)

        @block.gpsimd
        def _(pool):
            G = nc.gpsimd
            G.iota(slot_base_i[:, :], [[CAP, E]], base=1, channel_multiplier=0)
            G.iota(tok_i[:, :], [[P, 2]], base=DUMP, channel_multiplier=1)
            G.memset(ident[:, :], 0.0)
            G.memset(onesb[:, :], 1.0).then_inc(sem("pool_made"), 1)
            pool.wait_ge(sem("pool_made"), 1)
            G.affine_select(out=ident[:, :], in_=ident[:, :], compare_op=ALU.not_equal, fill=1.0, base=0,
                            pattern=[[-1, P]], channel_multiplier=1).then_inc(sem("pool_made"), 1)
            G.affine_select(out=strict_tri[:, :], in_=onesb[:, :], compare_op=ALU.is_gt, fill=0.0, base=0,
                            pattern=[[1, P]], channel_multiplier=-1).then_inc(sem("pool_made"), 1)
            phase_end(pool, 1)
            xe_v = xe.rearrange("(n e h p) c -> n p e h c", n=8, p=P, h=HALVES)
            for n in range(8):
                for h in range(HALVES):
                    G.dma_start(xe_v[n, :, :, h, :], zt[:, h, :].unsqueeze(1).broadcast_to([P, E // 8, ROW])).then_inc(sem("xe_zero"), 16)
                    pool.wait_ge(sem("xe_zero"), 16 * (HALVES * n + h + 1))
            for n in range(2):
                G.dma_start(acc[n][T:T + HALVES * P, :].rearrange("(n p) d -> p n d", p=P), zt[:, :, 0:D]
                            ).then_inc(sem("xe_zero"), 16)

            def scatter(k):
                if k is None:
                    return
                b, r = k
                pool.wait_ge(sem("slot_step_0"), 6 * b + 6)
                hold(pool)
                for n in range(TOPK):
                    G.indirect_dma_start(out=xe[:, :], out_offset=bass.IndirectOffsetOnAxis(ap=idx[r][:, n:n + 1], axis=0),
                                         in_=pay[r][:, :], in_offset=None, bounds_check=E * CAP - 1,
                                         oob_is_err=False).then_inc(sem(f"scattered{r}"), 16)

            attention_slots(pool, lambda stage: scatter(stage(5)))
            for r in range(4):
                pool.wait_ge(sem(f"scattered{r}"), 32 * NB)
            pool.wait_ge(sem("xe_zero"), 16 * (8 * HALVES + 2))
            phase_end(pool, 2)
            experts_pool(pool)
            phase_end(pool, 3)
            phase_end(pool, 4)
            ReduceOp = bass.bass_isa.ReduceOp
            pool.wait_ge(sem("amax_done"), 1)
            G.partition_all_reduce(gmax[:, 0:1], amax[:, 0:1], P, ReduceOp.max).then_inc(sem("gmax_done"), 1)
            pass0_pool(pool)
            phase_end(pool, 5)
            pool.wait_ge(sem("amax_done"), 2)
            G.partition_all_reduce(gmax[:, 1:2], amax[:, 1:2], P, ReduceOp.max).then_inc(sem("gmax_done"), 1)
            phase_end(pool, 6)
            pass1_pool(pool)

        @block.scalar
        def _(act):
            act.wait_ge(sem("w_in"), 16 * 16)
            nc.scalar.activation(tg[:, :], gates[:, :], ACT.Tanh).then_inc(sem("tg_done"), 1)
            phase_end(act, 1)
            attention_act(act, 0)
            phase_end(act, 2)
            experts_act(act)
            phase_end(act, 3)
            attention_act(act, 1)
            phase_end(act, 4)
            act.wait_ge(sem("clip_in"), 32)
            nc.scalar.activation(sig[:, :], clips[:, :], ACT.Exp, scale=-1.0).then_inc(sem("sig_done"), 1)
            weights_act(act)
            act.wait_ge(sem("sx_done"), 1)
            pass0_act(act)
            phase_end(act, 5)
            phase_end(act, 6)
            pass1_act(act)

        @block.tensor
        def _(pe):
            phase_end(pe, 1)
            attention_pe(pe, 0)
            phase_end(pe, 2)
            experts_pe(pe)
            phase_end(pe, 3)
            attention_pe(pe, 1)
            phase_end(pe, 4)
            weights_pe(pe)
            pass0_pe(pe)
            phase_end(pe, 5)
            phase_end(pe, 6)
            pass1_pe(pe)

        @block.vector
        def _(dve):
            V = nc.vector
            for k in range(2):
                V.memset(kbd[k][:, :, :], 0.0)
                V.memset(vx[k][:, :, DH:32], 0.0)
            V.memset(zt[:, :, :], 0.0)
            V.memset(count[:, :], 0.0)
            V.memset(gs[:, EG:EG + 4], LOW)
            V.memset(tog[:, GSEL:8], LOW)
            V.memset(mv[:, :, :], 1.0)
            for r in range(4):
                V.memset(pay[r][:, TOKC:ROW], 0.0)
            st = Steps(dve, "set_step", 3, 0)
            st.then(V.memset(amax[:, :], 0.0))
            for k in range(2):
                V.memset(vx[k][:, :, DH:DH + 1], 1.0)
            dve.wait_ge(sem("pool_made"), 3)
            V.tensor_copy(identb[:, :], ident[:, :])
            V.tensor_copy(slot_base[:, :], slot_base_i[:, :])
            st.then(V.tensor_copy(zt[:, :, TOKC], tok_i[:, :]))
            for r in range(4):
                V.tensor_scalar(pay[r][:, TOKC:TOKC + 1], zt[:, 0, TOKC:TOKC + 1], float((r - 4) * P - DUMP), None, ALU.add)
            dve.wait_ge(sem("w_in"), 16 * 16)
            st.then(V.tensor_scalar(mask_bias[:, :], mask_i[:, :], 0, NEG, ALU.is_equal, ALU.mult))
            dve.wait_ge(sem("tg_done"), 1)
            V.tensor_scalar(tg_half[:, :], tg[:, 2:3], 0.5, None, ALU.mult)
            V.tensor_scalar(tg_route[:, :], tg[:, 2:3], ROUTE_SCALE, None, ALU.mult)
            st.end()
            split_biases(dve, 0)
            phase_end(dve, 1)
            attention_dve(dve, 0)
            phase_end(dve, 2)
            experts_dve(dve)
            dve.wait_ge(sem("w_in"), 16 * 24)
            split_biases(dve, 1)
            phase_end(dve, 3)
            attention_dve(dve, 1)
            dve.wait_ge(sem("tmax_done"), NB)
            V.tensor_reduce(amax[:, 0:1], tmax[:, :], AX, ALU.max).then_inc(sem("amax_done"), 1)
            phase_end(dve, 4)
            if IREST:
                for n in range(2):
                    last = V.memset(wraw[n][IREST:P, IFULL, :], 0.0)
                last.then_inc(sem("pad_set"), 1)
                dve.wait_ge(sem("pad_set"), 1)
            weights_dve(dve)
            dve.wait_ge(sem("sx_done"), 1)
            V.tensor_copy(xq_f[0][:, 0:D].rearrange("p (c o) -> p c o", c=KC),
                          s_d[:, :].unsqueeze(2).broadcast_to([P, KC, P])).then_inc(sem("sd_wide"), 1)
            dve.wait_ge(sem("sd_t"), 1)
            V.tensor_copy(sd_row[:, :], bank[1][:, 0:D])
            pass0_dve(dve)
            dve.wait_ge(sem("f_max_done"), IC * NC_)
            V.tensor_reduce(amax[:, 1:2], hmax[:, :], AX, ALU.max).then_inc(sem("amax_done"), 1)
            phase_end(dve, 5)
            st = Steps(dve, "sh_step", 5, 0)
            dve.wait_ge(sem("gmax_done"), 2)
            st.then(V.tensor_scalar(scl[:, 2:3], gmax[:, 1:2], sig[:, 1:2], 1.0 / QMAX, ALU.mult, ALU.mult))
            st.then(V.reciprocal(scl[:, 3:4], scl[:, 2:3]))
            st.then(V.tensor_scalar(s_guq[:, :], s_gux[:, 1, :], scl[:, 3:4], None, ALU.mult))
            st.then(V.tensor_scalar(scl[:, 4:5], scl[:, 2:3], tg[:, 3:4], None, ALU.mult))
            st.then(V.tensor_scalar(sd_row[:, :], sd_row[:, :], scl[:, 4:5], None, ALU.mult))
            st.end()
            phase_end(dve, 6)
            pass1_dve(dve)


_TRANSPOSED = ("ctx_1024", "L0_xattn_wq_w", "L0_xattn_wk_w", "L0_xattn_wv_w", "L0_xattn_wo_w", "L0_ffn_gate_weight", "L0_ffn_w1",
               "L0_ffn_w2", "L0_ffn_w3", "L0_ffn_shared_gate", "L0_ffn_shared_up", "L0_ffn_shared_down",
               "L1_xattn_wq", "L1_xattn_wk", "L1_xattn_wv", "L1_xattn_wo")


def kernel(**inputs):
    import numpy as np
    import concourse.bacc as bacc
    from concourse.bass_utils import run_bass_kernel_spmd

    nc = bacc.Bacc("TRN2", target_bir_lowering=False, num_devices=1)
    arrays, aps = {}, {}
    for name, value in inputs.items():
        v = np.asarray(value)
        if name in _TRANSPOSED:
            v = np.swapaxes(v, -1, -2)
        v = np.ascontiguousarray(v)
        arrays[f"in_{name}"] = v
        aps[name] = nc.dram_tensor(f"in_{name}", v.shape, mybir.dt.from_np(v.dtype), kind="ExternalInput").ap()
    out = nc.dram_tensor("out_0", arrays["in_x"].shape, mybir.dt.float32, kind="ExternalOutput").ap()
    flamingo_gated_two_layers(nc, aps, out)
    result = run_bass_kernel_spmd(nc, [arrays], core_ids=[0])
    return result.results[0]["out_0"]
```
